# Optimizing a Trainium2 kernel written in Bass

```python
import numpy as np
import jax
import jax.numpy as jnp

def _softmax(x, axis=-1):
    return jax.nn.softmax(x, axis=axis)

def _gelu(x):
    return jax.nn.gelu(x, approximate=True)

def _silu(x):
    return jax.nn.silu(x)

def _sigmoid(x):
    return jax.nn.sigmoid(x)

def _layernorm(x, axis=-1, eps=1e-05):
    m = jnp.mean(x, axis=axis, keepdims=True)
    v = jnp.var(x, axis=axis, keepdims=True)
    return (x - m) / jnp.sqrt(v + eps)

def _scatter_add(tgt, idx, src, axis=0):
    return tgt.at[idx].add(src)

def _segment_sum(src, seg, n):
    return jax.ops.segment_sum(src, seg, n)
kernel_name = 'mk_macaron_d1_jaxref_r8_7ffc76'

def setup_inputs(seed: int=0):
    np.random.seed(seed)
    _w = jnp.asarray

    def _L0_attn_setup():
        import jax, jax.numpy as jnp
        import numpy as np
        B, L, R = (4, 256, 128)
        HID, EXP, K = (64, 2, 3)
        D = HID * EXP
        N = HID
        key = jax.random.key(seed)
        ks = jax.random.split(key, 16)
        g = lambda k, s: jax.random.normal(k, s, dtype=jnp.float32) * 0.02
        inp = {'up_x': jax.random.normal(ks[0], (B, L, R), dtype=jnp.float32), 'W_up': g(ks[1], (R, 2 * D)), 'b_up': g(ks[2], (2 * D,)), 'conv_w': g(ks[3], (D, K)), 'conv_b': g(ks[4], (D,)), 'W_delta': g(ks[5], (D, D)), 'b_delta': g(ks[6], (D,)), 'W_B': g(ks[7], (D, N)), 'b_B': g(ks[8], (N,)), 'W_C': g(ks[9], (D, N)), 'b_C': g(ks[10], (N,)), 'A_log': jnp.log(jnp.broadcast_to(jnp.arange(1, N + 1, dtype=jnp.float32), (D, N))), 'D_skip': jnp.ones((D,), dtype=jnp.float32), 'W_down': g(ks[11], (D, R)), 'b_down': g(ks[12], (R,))}
        return inp
    _L0_attn_in = _L0_attn_setup()

    def _L0_ffn_setup():
        import jax, jax.numpy as jnp
        import numpy as np
        H = 128
        I = 88
        E = 64
        TOP_K = 8
        NG = 8
        TOPK_GROUP = 4
        N_SHARED = 2
        ROUTED_SCALE = 2.5
        S_I = I * N_SHARED

        def _route(x, gate_w, gate_bias):
            T = x.shape[0]
            logits = x @ gate_w.T
            scores = jax.nn.sigmoid(logits)
            scores_for_choice = scores + gate_bias[None, :]
            grp = scores_for_choice.reshape(T, NG, E // NG)
            group_scores = jnp.sum(jax.lax.top_k(grp, 2)[0], axis=-1)
            _, gidx = jax.lax.top_k(group_scores, TOPK_GROUP)
            gmask = jnp.zeros((T, NG), dtype=scores.dtype).at[jnp.arange(T)[:, None], gidx].set(1.0)
            emask = jnp.repeat(gmask, E // NG, axis=1)
            masked = jnp.where(emask > 0, scores_for_choice, 0.0)
            _, topk_idx = jax.lax.top_k(masked, TOP_K)
            topk_w = jnp.take_along_axis(scores, topk_idx, axis=1)
            topk_w = topk_w / (jnp.sum(topk_w, axis=-1, keepdims=True) + 1e-20)
            topk_w = topk_w * ROUTED_SCALE
            rw = jnp.zeros((T, E), dtype=scores.dtype).at[jnp.arange(T)[:, None], topk_idx].add(topk_w)
            return rw

        def _mlp(x, gw, uw, dw):
            return jax.nn.silu(x @ gw.T) * (x @ uw.T) @ dw.T
        key = jax.random.key(seed)
        ks = jax.random.split(key, 10)
        sc = 0.02
        return {'hidden_states': jax.random.normal(ks[0], (1, 128, H), dtype=jnp.float32), 'gate_w': sc * jax.random.normal(ks[1], (E, H), dtype=jnp.float32), 'gate_bias': sc * jax.random.normal(ks[2], (E,), dtype=jnp.float32), 'Wg': sc * jax.random.normal(ks[3], (E, I, H), dtype=jnp.float32), 'Wu': sc * jax.random.normal(ks[4], (E, I, H), dtype=jnp.float32), 'Wd': sc * jax.random.normal(ks[5], (E, H, I), dtype=jnp.float32), 'Sg': sc * jax.random.normal(ks[6], (S_I, H), dtype=jnp.float32), 'Su': sc * jax.random.normal(ks[7], (S_I, H), dtype=jnp.float32), 'Sd': sc * jax.random.normal(ks[8], (H, S_I), dtype=jnp.float32)}
    _L0_ffn_in = _L0_ffn_setup()
    _d = {'L0_attn_up_x': _L0_attn_in['up_x'], 'L0_attn_W_up': _L0_attn_in['W_up'], 'L0_attn_b_up': _L0_attn_in['b_up'], 'L0_attn_conv_w': _L0_attn_in['conv_w'], 'L0_attn_conv_b': _L0_attn_in['conv_b'], 'L0_attn_W_delta': _L0_attn_in['W_delta'], 'L0_attn_b_delta': _L0_attn_in['b_delta'], 'L0_attn_W_B': _L0_attn_in['W_B'], 'L0_attn_b_B': _L0_attn_in['b_B'], 'L0_attn_W_C': _L0_attn_in['W_C'], 'L0_attn_b_C': _L0_attn_in['b_C'], 'L0_attn_A_log': _L0_attn_in['A_log'], 'L0_attn_D_skip': _L0_attn_in['D_skip'], 'L0_attn_W_down': _L0_attn_in['W_down'], 'L0_attn_b_down': _L0_attn_in['b_down'], 'L0_ffn_gate_w': _L0_ffn_in['gate_w'], 'L0_ffn_gate_bias': _L0_ffn_in['gate_bias'], 'L0_ffn_Wg': _L0_ffn_in['Wg'], 'L0_ffn_Wu': _L0_ffn_in['Wu'], 'L0_ffn_Wd': _L0_ffn_in['Wd'], 'L0_ffn_Sg': _L0_ffn_in['Sg'], 'L0_ffn_Su': _L0_ffn_in['Su'], 'L0_ffn_Sd': _L0_ffn_in['Sd']}
    _x0 = _d['L0_attn_up_x']
    _d['L0_attn_up_x'] = jax.random.normal(jax.random.fold_in(jax.random.key(seed), 1), (4, 1024, 128), dtype=_x0.dtype)
    del _x0
    return _d

def reference(L0_attn_up_x, L0_attn_W_up, L0_attn_b_up, L0_attn_conv_w, L0_attn_conv_b, L0_attn_W_delta, L0_attn_b_delta, L0_attn_W_B, L0_attn_b_B, L0_attn_W_C, L0_attn_b_C, L0_attn_A_log, L0_attn_D_skip, L0_attn_W_down, L0_attn_b_down, L0_ffn_gate_w, L0_ffn_gate_bias, L0_ffn_Wg, L0_ffn_Wu, L0_ffn_Wd, L0_ffn_Sg, L0_ffn_Su, L0_ffn_Sd):

    def _L0_attn_ref(up_x, W_up, b_up, conv_w, conv_b, W_delta, b_delta, W_B, b_B, W_C, b_C, A_log, D_skip, W_down, b_down):
        import jax, jax.numpy as jnp
        import numpy as np
        B, L, R = (4, 256, 128)
        HID, EXP, K = (64, 2, 3)
        D = HID * EXP
        N = HID
        Lq = up_x.shape[1]
        u = up_x @ W_up + b_up
        left, right = jnp.split(u, 2, axis=-1)
        xp = jnp.pad(left, ((0, 0), (K - 1, 0), (0, 0)))
        conv = sum((conv_w[:, k] * xp[:, k:k + Lq, :] for k in range(K))) + conv_b
        x = jax.nn.silu(conv)
        delta = jax.nn.softplus(x @ W_delta + b_delta)
        Bm = x @ W_B + b_B
        Cm = x @ W_C + b_C
        A = -jnp.exp(A_log)
        dA = jnp.exp(delta[..., None] * A)
        dBx = delta[..., None] * Bm[:, :, None, :] * x[..., None]

        def step(h, inputs):
            dA_t, dBx_t, C_t = inputs
            h = dA_t * h + dBx_t
            y_t = jnp.einsum('bdn,bn->bd', h, C_t)
            return (h, y_t)
        h0 = jnp.zeros((up_x.shape[0], D, N), dtype=x.dtype)
        _, ys = jax.lax.scan(step, h0, (jnp.swapaxes(dA, 0, 1), jnp.swapaxes(dBx, 0, 1), jnp.swapaxes(Cm, 0, 1)))
        y = jnp.swapaxes(ys, 0, 1) + D_skip * x
        gated = y * jax.nn.silu(right)
        return gated @ W_down + b_down

    def _L0_ffn_ref(hidden_states, gate_w, gate_bias, Wg, Wu, Wd, Sg, Su, Sd):
        import jax, jax.numpy as jnp
        import numpy as np
        H = 128
        I = 88
        E = 64
        TOP_K = 8
        NG = 8
        TOPK_GROUP = 4
        N_SHARED = 2
        ROUTED_SCALE = 2.5
        S_I = I * N_SHARED

        def _route(x, gate_w, gate_bias):
            T = x.shape[0]
            logits = x @ gate_w.T
            scores = jax.nn.sigmoid(logits)
            scores_for_choice = scores + gate_bias[None, :]
            grp = scores_for_choice.reshape(T, NG, E // NG)
            group_scores = jnp.sum(jax.lax.top_k(grp, 2)[0], axis=-1)
            _, gidx = jax.lax.top_k(group_scores, TOPK_GROUP)
            gmask = jnp.zeros((T, NG), dtype=scores.dtype).at[jnp.arange(T)[:, None], gidx].set(1.0)
            emask = jnp.repeat(gmask, E // NG, axis=1)
            masked = jnp.where(emask > 0, scores_for_choice, 0.0)
            _, topk_idx = jax.lax.top_k(masked, TOP_K)
            topk_w = jnp.take_along_axis(scores, topk_idx, axis=1)
            topk_w = topk_w / (jnp.sum(topk_w, axis=-1, keepdims=True) + 1e-20)
            topk_w = topk_w * ROUTED_SCALE
            rw = jnp.zeros((T, E), dtype=scores.dtype).at[jnp.arange(T)[:, None], topk_idx].add(topk_w)
            return rw

        def _mlp(x, gw, uw, dw):
            return jax.nn.silu(x @ gw.T) * (x @ uw.T) @ dw.T
        B, S, _ = hidden_states.shape
        x = hidden_states.reshape(B * S, H)
        rw = _route(x, gate_w, gate_bias)
        expert_out = jax.vmap(lambda gw_, uw_, dw_: _mlp(x, gw_, uw_, dw_))(Wg, Wu, Wd)
        routed = jnp.einsum('eth,te->th', expert_out, rw)
        shared = _mlp(x, Sg, Su, Sd)
        out = (routed + shared).reshape(B, S, H)
        return out
    x = L0_attn_up_x
    x = x + 0.5 * _L0_ffn_ref(_layernorm(x, axis=-1), L0_ffn_gate_w, L0_ffn_gate_bias, L0_ffn_Wg, L0_ffn_Wu, L0_ffn_Wd, L0_ffn_Sg, L0_ffn_Su, L0_ffn_Sd)
    x = x + _L0_attn_ref(_layernorm(x, axis=-1), L0_attn_W_up, L0_attn_b_up, L0_attn_conv_w, L0_attn_conv_b, L0_attn_W_delta, L0_attn_b_delta, L0_attn_W_B, L0_attn_b_B, L0_attn_W_C, L0_attn_b_C, L0_attn_A_log, L0_attn_D_skip, L0_attn_W_down, L0_attn_b_down)
    x = x + 0.5 * _L0_ffn_ref(_layernorm(x, axis=-1), L0_ffn_gate_w, L0_ffn_gate_bias, L0_ffn_Wg, L0_ffn_Wu, L0_ffn_Wd, L0_ffn_Sg, L0_ffn_Su, L0_ffn_Sd)
    return x

_drawn_inputs = setup_inputs


def setup_inputs(seed=0):
    import zlib

    import numpy as np

    out = dict(_drawn_inputs(seed))
    spreads = {'L0_attn_D_skip': (1.0, 0.6)}
    factors = {'L0_attn_W_up': 8.0,
     'L0_attn_b_up': 8.0,
     'L0_attn_conv_w': 8.0,
     'L0_attn_conv_b': 8.0,
     'L0_attn_W_delta': 8.0,
     'L0_attn_b_delta': 8.0,
     'L0_attn_W_B': 8.0,
     'L0_attn_b_B': 8.0,
     'L0_attn_W_C': 8.0,
     'L0_attn_b_C': 8.0,
     'L0_attn_A_log': 8.0,
     'L0_attn_W_down': 8.0,
     'L0_attn_b_down': 3.052,
     'L0_ffn_gate_w': 8.0,
     'L0_ffn_gate_bias': 8.0,
     'L0_ffn_Wg': 8.0,
     'L0_ffn_Wu': 8.0,
     'L0_ffn_Wd': 8.0,
     'L0_ffn_Sg': 8.0,
     'L0_ffn_Su': 8.0,
     'L0_ffn_Sd': 8.0}
    for name, (base, spread) in spreads.items():
        noise = np.random.default_rng([zlib.crc32(name.encode()), seed]).standard_normal(out[name].shape)
        drawn = base * np.exp(spread * noise) if base else spread * noise
        out[name] = jnp.asarray(drawn.astype(out[name].dtype))
    for name, factor in factors.items():
        out[name] = (out[name] * factor).astype(out[name].dtype)
    return out
```

```python
from contextlib import ExitStack

import concourse.bass as bass
from concourse import mybir

F32 = mybir.dt.float32
F16 = mybir.dt.float16
ALU = mybir.AluOpType
ACT = mybir.ActivationFunctionType
AX_X = mybir.AxisListType.X
ds = bass.ds

P = 128
BATCH, SEQ = 4, 1024
TOKENS = BATCH * SEQ
BLK = 512
NBLK = TOKENS // BLK
HALVES = SEQ // BLK
SUB = BLK // P
STATE = 64
TAPS = 3
EXPERTS, INNER, SHARED = 64, 88, 176
GROUPS, KEEP_GROUPS, TOPK = 8, 4, 8
PER_GROUP = EXPERTS // GROUPS
ROUTED_ROWS = EXPERTS * INNER
ROWS = ROUTED_ROWS + SHARED
ROUTED_TILES = ROUTED_ROWS // P
TILES = -(-ROWS // P)
LAST = ROWS - (TILES - 1) * P
ROUTED_SCALE = 2.5
EPS = 1e-5
WS = 64.0
PAD = 1e30
GONE = -1e30
GPAD = GROUPS + KEEP_GROUPS

V_UPL, V_UPR, V_TAP, V_CONV, V_DELTA, V_B, V_C, V_SKIP, V_DOWN = 0, 1, 2, 5, 6, 7, 8, 9, 10
NVEC = 11


def macaron(nc, x_in, w_up, w_delta, w_b2, w_c2, w_down, vecs_in, a_log, gate_wt, gate_bias,
            wg_in, wu_in, wd_in, wd_last, row_of_expert_in, one_hot_in, eye_in, eye16_in, out):
    ctx = ExitStack()
    with ctx:
        def sb(name, shape, dt=F32):
            return ctx.enter_context(nc.sbuf_tensor(name, shape, dt))

        def sem(name):
            return ctx.enter_context(nc.semaphore(name))

        x = sb("x", [P, TOKENS])
        wg = [sb(f"wg_{k}", [P, TILES * P], F16) for k in ("high", "low")]
        wu = [sb(f"wu_{k}", [P, TILES * P], F16) for k in ("high", "low")]
        wd = [sb(f"wd_{k}", [P, TILES * P], F16) for k in ("high", "low")]
        row_of_expert = sb("row_of_expert", [P, ROUTED_ROWS], F16)
        F1 = sb("F1", [P, TOKENS])
        F2 = sb("F2", [P, BATCH * (SEQ + TAPS - 1)])
        F3 = sb("F3", [P, TOKENS])
        F4 = sb("F4", [P, TOKENS])
        xh = F1[:, :].bitcast(F16)
        rwt = F2[:, :].bitcast(F16)
        normed, delta = F1, F1
        left, dx = F2, F2
        conv_x = F3
        gate = F4
        bs = sb("b_halves", [P, TOKENS], F16)
        cs = sb("c_halves", [P, TOKENS], F16)
        arena = sb("arena", [P, 6 * SEQ])
        silu_g = [arena[:, k * BLK:(k + 1) * BLK] for k in range(2)]
        prod = [arena[:, (2 + k) * BLK:(3 + k) * BLK] for k in range(2)]
        hid = [arena[:, (4 + k) * BLK:(5 + k) * BLK] for k in range(2)]
        halves = arena[:, 6 * BLK:8 * BLK].bitcast(F16)
        hid_hi = [halves[:, k * BLK:(k + 1) * BLK] for k in range(2)]
        hid_lo = [halves[:, (2 + k) * BLK:(3 + k) * BLK] for k in range(2)]
        decay = [arena[:, k * SEQ:(k + 1) * SEQ] for k in range(2)]
        c_row = [arena[:, (2 + k) * SEQ:(3 + k) * SEQ] for k in range(2)]
        state = [arena[:, (4 + k) * SEQ:(5 + k) * SEQ] for k in range(2)]
        term = [row_of_expert[:, :].bitcast(F32)[:, k * SEQ:(k + 1) * SEQ] for k in range(2)]

        w_up_sb = sb("w_up_sb", [P, 2 * P])
        w_delta_sb = sb("w_delta_sb", [P, P])
        w_b_sb = sb("w_b_sb", [P, P])
        w_c_sb = sb("w_c_sb", [P, P])
        w_down_sb = sb("w_down_sb", [P, P])
        vecs = sb("vecs", [P, NVEC])
        a_neg = sb("a_neg", [P, STATE])
        gate_w_sb = sb("gate_w_sb", [P, EXPERTS])
        gate_b_sb = sb("gate_b_sb", [P, EXPERTS])
        one_hot = sb("one_hot", [P, STATE], F16)
        eye = sb("eye", [P, P])
        eye16 = sb("eye16", [P, P], F16)
        mean_w = sb("mean_w", [P, P])
        eps_col = sb("eps_col", [P, 1])

        NE = SUB * EXPERTS
        NG = SUB * GROUPS
        cf, bf = cs[:, :].bitcast(F32), bs[:, :].bitcast(F32)
        cent, sq, xn = [cf[:, k * BLK:(k + 1) * BLK] for k in range(3)]
        expo, score, choice, rest = [bf[:, k * NE:(k + 1) * NE] for k in range(4)]
        hi4, lo4 = [bf[:, (4 * NE + k * NG * 4):(4 * NE + (k + 1) * NG * 4)] for k in range(2)]
        mn, ml = [bf[:, (5 * NE + k * NG * 2):(5 * NE + (k + 1) * NG * 2)] for k in range(2)]
        rwp = bs[:, 12 * NE:14 * NE].rearrange("p (t e) -> p t e", t=SUB)
        top8 = sb("top8", [P, 2, SUB, 8])
        gscore = sb("gscore", [P, SUB, GPAD])
        gleft = sb("gleft", [P, SUB, GPAD])
        gmask = sb("gmask", [P, NG])
        denom = sb("denom", [P, SUB])

        bank = ctx.enter_context(nc.psum_tensor("bank", [P, 8, BLK], F32))

        s_x = sem("x_loaded")
        s_small = sem("small_loaded")
        s_row = sem("row_table_loaded")
        s_stage = [sem(f"stage_loaded{k}") for k in range(4)]
        s_split = sem("weights_split")
        s_const = sem("constants_set")
        s_aneg = sem("a_neg_ready")
        s_out = sem("out_stored")
        s_mean, s_cent, s_sq, s_var, s_rstd, s_xn = map(sem, (
            "mean_ready", "centred", "squared", "var_ready", "rstd_ready", "normed"))
        s_ln = sem("log_var")
        s_xhi, s_xlo = sem("x_high"), sem("x_low")
        s_logit, s_expo, s_rwp, s_rwt_ps, s_rwt = map(sem, (
            "logits_ready", "exp_ready", "routing_ready", "routing_transposed", "routing_stored"))
        s_vec = sem("vector_chain")
        s_g, s_u, s_rw, s_silu, s_prod, s_hid, s_hhi, s_hlo, s_dn, s_xadd = map(sem, (
            "gate_rows", "up_rows", "weight_rows", "silu_ready", "product_ready", "hidden_ready",
            "hidden_high", "hidden_low", "down_done", "x_updated"))
        s_l, s_r, s_lsb, s_gate, s_conv, s_x1, s_zd, s_zb, s_zc, s_abs, s_e, s_sp, s_rel, s_dl, s_dxs, \
            s_bh, s_ch, s_bl = map(sem, (
                "left_rows", "right_rows", "left_stored", "gate_stored", "conv_ready", "conv_x_ready",
                "delta_rows", "b_rows", "c_rows", "abs_ready", "exp_abs_ready", "log1p_ready", "relu_ready",
                "delta_ready", "dx_ready", "b_high", "c_high", "bc_low"))
        s_taps = sem("conv_chain")
        s_pad = sem("left_padded")
        s_bps, s_cps, s_dec, s_crow, s_dbx, s_scan, s_term, s_yacc, s_skip, s_gated = map(sem, (
            "b_spread", "c_spread", "decay_ready", "c_copied", "dbx_ready", "scan_done", "term_ready",
            "term_added", "y_skip", "gated_ready"))
        s_mix, s_xmix = sem("mixer_rows"), sem("x_mixed")

        s_pass = sem("passed")
        s_whi = sem("weight_highs_made")
        CREDIT = {s_cent: 1, s_silu: 2, s_prod: 2, s_hid: 2, s_hlo: 2, s_dn: 2, s_xadd: 1, s_xlo: 1,
                  s_lsb: 2, s_gate: 2, s_rel: 2, s_bl: 4, s_dl: 1, s_scan: 2, s_crow: 1, s_term: 2,
                  s_yacc: 2, s_skip: 1, s_xmix: 2, s_x1: 1, s_xn: 1}

        def done(s, i):
            return CREDIT[s] + i + 1

        chunks = []
        for w, src, n in ((wg, wg_in, ROWS // 3), (wu, wu_in, ROWS // 3), (wd, wd_in, (TILES - 1) * P // 3)):
            for c in range(3):
                chunks.append((w, c * n, n, src[:, c * n:(c + 1) * n], P))
        chunks.append((wd, (TILES - 1) * P, P, wd_last, LAST))
        stage_of = [(F3, 0), (F3, 2048), (F4, 0), (F4, 2048)]

        def stage(c):
            buf, at = stage_of[c % 4]
            return buf[0:chunks[c][4], at:at + chunks[c][2]]

        block = ctx.enter_context(nc.Block())

        @block.sync
        def _(sp):
            for k in range(4):
                w = TOKENS // 4
                sp.dma_start(x[:, k * w:(k + 1) * w], x_in[:, k * w:(k + 1) * w]).then_inc(s_x, 16)
            for dst, src in ((gate_w_sb, gate_wt), (gate_b_sb, gate_bias), (eye16, eye16_in), (vecs, vecs_in),
                             (a_neg, a_log), (w_up_sb, w_up), (w_delta_sb, w_delta), (w_b_sb, w_b2),
                             (w_c_sb, w_c2), (w_down_sb, w_down), (one_hot, one_hot_in), (eye, eye_in)):
                sp.dma_start(dst[:, :], src).then_inc(s_small, 16)
            for c, (w, at, n, src, rows) in enumerate(chunks):
                if c >= 4:
                    sp.wait_ge(s_split, c - 4 + 1)
                sp.dma_start(stage(c), src).then_inc(s_stage[c % 4], 16)
                if c == 3:
                    sp.dma_start(row_of_expert[:, :], row_of_expert_in).then_inc(s_row, 16)
            sp.wait_ge(s_yacc, done(s_yacc, BATCH * STATE - 1))
            sp.dma_start(row_of_expert[:, :], row_of_expert_in).then_inc(s_row, 16)
            with sp.Fori(0, NBLK) as blk:
                sp.wait_ge(s_xadd, done(s_xadd, NBLK + blk))
                sp.dma_start(out[:, ds(blk * BLK, BLK)], x[:, ds(blk * BLK, BLK)]).then_inc(s_out, 16)
            sp.wait_ge(s_out, 16 * NBLK)

        SMALL = 16 * 12
        NCONST = 9

        @block.tensor
        def _(pe):
            for s in (s_dn, s_yacc):
                pe.sem_inc(s, CREDIT[s])

            def mm(dst, lhsT, rhs, start=True, stop=True):
                return pe.matmul(dst, lhsT, rhs, start=start, stop=stop)

            def norm(blk, n):
                pe.wait_ge(s_cent, n + 1)
                mm(bank[:, 0, :], mean_w[:, :], x[:, ds(blk * BLK, BLK)]).then_inc(s_mean, 1)
                pe.wait_ge(s_sq, n + 1)
                mm(bank[:, 1, :], mean_w[:, :], sq[:, :]).then_inc(s_var, 1)

            def route(n, r):
                pe.wait_ge(s_xn, done(s_xn, n))
                for t in range(SUB):
                    i = mm(bank[:, 2, t * EXPERTS:(t + 1) * EXPERTS], xn[:, t * P:(t + 1) * P], gate_w_sb[:, :])
                i.then_inc(s_logit, 1)
                pe.wait_ge(s_rwp, r + 1)
                dst = bank[:, 3, 0:BLK // 2].bitcast(F16)
                for t in range(SUB):
                    i = pe.transpose(dst[:, t * P:(t + 1) * P], rwp[:, t, :], eye16[:, :])
                i.then_inc(s_rwt_ps, 1)

            def rows(blk, j, u, k, routed=True):
                hi, lo = xh[:, ds(blk * BLK, BLK)], xh[:, ds(blk * BLK + TOKENS, BLK)]

                def product(dst, w):
                    wh, wl = w[0][:, ds(j * P, P)], w[1][:, ds(j * P, P)]
                    mm(dst, wh, hi, True, False)
                    mm(dst, wh, lo, False, False)
                    return mm(dst, wl, hi, False, True)
                pe.wait_ge(s_silu, u + 1)
                product(bank[:, k, :], wg).then_inc(s_g, 1)
                pe.wait_ge(s_prod, u + 1)
                product(bank[:, 2 + k, :], wu).then_inc(s_u, 1)
                pe.wait_ge(s_hid, u + 1)
                if routed:
                    mm(bank[:, 4 + k, :], row_of_expert[:, ds(j * P, P)], rwt[:, ds(blk * BLK, BLK)])\
                        .then_inc(s_rw, 1)

            def down(j, u, k, start=False, stop=False):
                pe.wait_ge(s_hlo, done(s_hlo, u))
                wh, wl = wd[0][:, ds(j * P, P)], wd[1][:, ds(j * P, P)]
                mm(bank[:, 6, :], wh, hid_hi[k], start, False)
                mm(bank[:, 6, :], wh, hid_lo[k], False, False)
                i = mm(bank[:, 6, :], wl, hid_hi[k], False, stop)
                i.then_inc(s_dn, 1)

            def ffn(layer):
                with pe.Fori(0, NBLK) as blk:
                    norm(blk, (2 * layer) * NBLK + blk)
                    route((2 * layer) * NBLK + blk, layer * NBLK + blk)
                if layer == 0:
                    pe.wait_ge(s_split, len(chunks))
                pe.wait_ge(s_row, 16 * (layer + 1))
                pe.wait_ge(s_rwt, (layer + 1) * NBLK)
                pe.wait_ge(s_xlo, done(s_xlo, (layer + 1) * NBLK - 1))
                base = layer * NBLK * TILES

                def tiles(blk, last=False):
                    u = base + blk * TILES
                    rows(blk, 2, u + 2, 0)
                    pe.wait_ge(s_xadd, layer * NBLK + blk + 1)
                    down(0, u, 0, start=True)
                    rows(blk, 3, u + 3, 1)
                    down(1, u + 1, 1)
                    with pe.Fori(2, ROUTED_TILES // 2) as p:
                        for k in range(2):
                            rows(blk, 2 * p + k, u + 2 * p + k, k)
                            down(2 * p + k - 2, u + 2 * p + k - 2, k)
                    for j in range(ROUTED_TILES, TILES):
                        rows(blk, j, u + j, j % 2, routed=False)
                        down(j - 2, u + j - 2, j % 2)
                    for k in range(2):
                        if not last:
                            rows(blk + 1, k, u + TILES + k, k)
                        down(TILES - 2 + k, u + TILES - 2 + k, k, stop=(k == 1))
                for k in range(2):
                    rows(0, k, base + k, k)
                with pe.Fori(0, NBLK - 1) as blk:
                    tiles(blk)
                tiles(NBLK - 1, last=True)

            def mixer():
                with pe.Fori(0, NBLK) as blk:
                    norm(blk, NBLK + blk)
                pe.wait_ge(s_xn, done(s_xn, 2 * NBLK - 1))
                with pe.Fori(0, BATCH) as b:
                    for h in range(HALVES):
                        n = b * HALVES + h
                        src = normed[:, ds(b * SEQ + h * BLK, BLK)]
                        pe.wait_ge(s_lsb, n + 1)
                        mm(bank[:, h, :], w_up_sb[:, 0:P], src).then_inc(s_l, 1)
                        pe.wait_ge(s_gate, n + 1)
                        mm(bank[:, 2 + h, :], w_up_sb[:, P:2 * P], src).then_inc(s_r, 1)
                pe.wait_ge(s_lsb, done(s_lsb, NBLK - 1))
                pe.wait_ge(s_gate, done(s_gate, NBLK - 1))
                with pe.Fori(0, BATCH) as b:
                    for h in range(HALVES):
                        n = b * HALVES + h
                        src = conv_x[:, ds(b * SEQ + h * BLK, BLK)]
                        pe.wait_ge(s_x1, done(s_x1, b))
                        pe.wait_ge(s_rel, n + 1)
                        mm(bank[:, h, :], w_delta_sb[:, :], src).then_inc(s_zd, 1)
                        pe.wait_ge(s_bl, 2 * n + 1)
                        mm(bank[:, 2 + h, :], w_b_sb[:, :], src).then_inc(s_zb, 1)
                        pe.wait_ge(s_bl, 2 * n + 2)
                        mm(bank[:, 4 + h, :], w_c_sb[:, :], src).then_inc(s_zc, 1)

                pe.wait_ge(s_bl, done(s_bl, 2 * NBLK - 1))
                pe.wait_ge(s_rel, done(s_rel, NBLK - 1))

                def spread(b, n, k):
                    u = b * STATE + n
                    sel = one_hot[:, ds(n, 1)].broadcast_to([P, P])
                    pe.wait_ge(s_scan, u + 1)
                    for h in range(HALVES):
                        i = mm(bank[:, 2 * k + h, :], sel, bs[:, ds(b * SEQ + h * BLK, BLK)])
                    i.then_inc(s_bps, 1)
                    pe.wait_ge(s_crow, u + 1)
                    for h in range(HALVES):
                        i = mm(bank[:, 4 + h, :], sel, cs[:, ds(b * SEQ + h * BLK, BLK)])
                    i.then_inc(s_cps, 1)

                def add_term(u, k, start=False, stop=False):
                    pe.wait_ge(s_term, done(s_term, u))
                    for h in range(HALVES):
                        i = mm(bank[:, 6 + h, :], eye[:, :], term[k][:, h * BLK:(h + 1) * BLK], start, stop)
                    i.then_inc(s_yacc, 1)
                    return i

                with pe.Fori(0, BATCH) as b:
                    u = b * STATE
                    spread(b, 0, 0)
                    spread(b, 1, 1)
                    spread(b, 2, 0)
                    pe.wait_ge(s_skip, b + 1)
                    add_term(u, 0, start=True)
                    spread(b, 3, 1)
                    add_term(u + 1, 1)
                    with pe.Fori(2, STATE // 2) as p:
                        for k in range(2):
                            spread(b, 2 * p + k, k)
                            add_term(u + 2 * p + k - 2, k)
                    add_term(u + STATE - 2, 0)
                    add_term(u + STATE - 1, 1, stop=True)
                with pe.Fori(0, BATCH) as b:
                    for h in range(HALVES):
                        pe.wait_ge(s_gated, b + 1)
                        pe.wait_ge(s_xmix, b * HALVES + h + 1)
                        mm(bank[:, h, :], w_down_sb[:, :], gate[:, ds(b * SEQ + h * BLK, BLK)]).then_inc(s_mix, 1)

            pe.wait_ge(s_x, 64)
            pe.wait_ge(s_small, SMALL)
            pe.wait_ge(s_const, NCONST)
            ffn(0)
            pe.wait_ge(s_xadd, NBLK + 1)
            mixer()
            pe.wait_ge(s_xmix, 2 + NBLK)
            ffn(1)

        @block.scalar
        def _(act):
            for s in (s_silu, s_lsb, s_gate, s_rel, s_crow, s_x1):
                act.sem_inc(s, CREDIT[s])

            def norm(n):
                act.wait_ge(s_cent, done(s_cent, n))
                act.activation(sq[:, :], cent[:, :], ACT.Square).then_inc(s_sq, 1)
                act.wait_ge(s_var, n + 1)
                act.activation(sq[:, :], bank[:, 1, :], ACT.Ln, bias=eps_col[:, :]).then_inc(s_ln, 1)
                act.wait_ge(s_ln, n + 1)
                act.activation(sq[:, :], sq[:, :], ACT.Exp, scale=-0.5).then_inc(s_rstd, 1)

            def route(blk, n, r):
                act.wait_ge(s_xn, done(s_xn, n))
                act.activation(xh[:, ds(blk * BLK, BLK)], xn[:, :], ACT.Copy).then_inc(s_xhi, 1)
                act.wait_ge(s_logit, r + 1)
                act.activation(expo[:, :], bank[:, 2, 0:NE], ACT.Exp, scale=-1.0).then_inc(s_expo, 1)
                act.wait_ge(s_rwt_ps, r + 1)
                act.activation(rwt[:, ds(blk * BLK, BLK)], bank[:, 3, 0:BLK // 2].bitcast(F16), ACT.Copy)\
                    .then_inc(s_rwt, 1)

            def silu(u, k):
                act.wait_ge(s_g, u + 1)
                act.wait_ge(s_prod, u + 1)
                act.activation(silu_g[k], bank[:, k, :], ACT.Silu, scale=1.0 / WS).then_inc(s_silu, 1)

            def high(u, k):
                act.wait_ge(s_hid, done(s_hid, u))
                act.wait_ge(s_dn, u + 1)
                act.activation(hid_hi[k], hid[k], ACT.Copy).then_inc(s_hhi, 1)

            def ffn(layer):
                act.preload_act_table_set("natural_log_exp_and_others")
                with act.Fori(0, NBLK) as blk:
                    norm(2 * layer * NBLK + blk)
                    route(blk, 2 * layer * NBLK + blk, layer * NBLK + blk)
                if layer == 0:
                    for c, (w, at, n, src, rows) in enumerate(chunks):
                        act.wait_ge(s_stage[c % 4], 16 * (c // 4 + 1))
                        act.activation(w[0][0:rows, at:at + n], stage(c), ACT.Copy, scale=WS).then_inc(s_whi, 1)
                act.preload_act_table_set("silu_and_others")
                base = layer * NBLK * TILES
                silu(base, 0)
                with act.Fori(0, NBLK * TILES // 2 - 1) as p:
                    u = base + 2 * p
                    silu(u + 1, 1)
                    high(u, 0)
                    silu(u + 2, 0)
                    high(u + 1, 1)
                u = base + NBLK * TILES - 2
                silu(u + 1, 1)
                high(u, 0)
                high(u + 1, 1)

            def mixer():
                act.preload_act_table_set("natural_log_exp_and_others")
                act.activation(a_neg[:, :], a_neg[:, :], ACT.Exp).then_inc(s_aneg, 1)
                with act.Fori(0, NBLK) as blk:
                    norm(NBLK + blk)
                act.preload_act_table_set("silu_and_others")
                act.wait_ge(s_pad, 1)
                with act.Fori(0, BATCH) as b:
                    for h in range(HALVES):
                        n = b * HALVES + h
                        act.wait_ge(s_l, n + 1)
                        act.activation(left[:, ds(b * (SEQ + TAPS - 1) + TAPS - 1 + h * BLK, BLK)], bank[:, h, :],
                                       ACT.Identity, bias=vecs[:, V_UPL:V_UPL + 1]).then_inc(s_lsb, 1)
                    for h in range(HALVES):
                        n = b * HALVES + h
                        act.wait_ge(s_r, n + 1)
                        act.activation(gate[:, ds(b * SEQ + h * BLK, BLK)], bank[:, 2 + h, :], ACT.Silu,
                                       bias=vecs[:, V_UPR:V_UPR + 1]).then_inc(s_gate, 1)
                    act.wait_ge(s_conv, b + 1)
                    act.activation(conv_x[:, ds(b * SEQ, SEQ)], state[0], ACT.Silu,
                                   bias=vecs[:, V_CONV:V_CONV + 1]).then_inc(s_x1, 1)
                act.preload_act_table_set("natural_log_exp_and_others")
                with act.Fori(0, BATCH) as b:
                    for h in range(HALVES):
                        n = b * HALVES + h
                        bias = vecs[:, V_DELTA:V_DELTA + 1]
                        at = b * SEQ + h * BLK
                        act.wait_ge(s_zd, n + 1)
                        act.wait_ge(s_dl, n + 1)
                        act.activation(decay[0][:, 0:BLK], bank[:, h, :], ACT.Abs, bias=bias).then_inc(s_abs, 1)
                        act.wait_ge(s_abs, n + 1)
                        act.activation(decay[0][:, 0:BLK], decay[0][:, 0:BLK], ACT.Exp, scale=-1.0).then_inc(s_e, 1)
                        act.wait_ge(s_e, n + 1)
                        act.activation(decay[0][:, 0:BLK], decay[0][:, 0:BLK], ACT.Ln, bias=1.0).then_inc(s_sp, 1)
                        act.activation(decay[1][:, 0:BLK], bank[:, h, :], ACT.Relu, bias=bias).then_inc(s_rel, 1)
                        act.wait_ge(s_zb, n + 1)
                        act.activation(bs[:, ds(at, BLK)], bank[:, 2 + h, :], ACT.Identity,
                                       bias=vecs[:, V_B:V_B + 1]).then_inc(s_bh, 1)
                        act.wait_ge(s_zc, n + 1)
                        act.activation(cs[:, ds(at, BLK)], bank[:, 4 + h, :], ACT.Identity,
                                       bias=vecs[:, V_C:V_C + 1]).then_inc(s_ch, 1)
                act.wait_ge(s_aneg, 2)
                act.wait_ge(s_dl, 1 + NBLK)
                with act.Fori(0, BATCH) as b:
                    with act.Fori(0, STATE // 2) as p:
                        for k in range(2):
                            u = b * STATE + 2 * p + k
                            act.wait_ge(s_scan, u + 1)
                            act.activation(decay[k], delta[:, ds(b * SEQ, SEQ)], ACT.Exp,
                                           scale=a_neg[:, ds(2 * p + k, 1)]).then_inc(s_dec, 1)
                            act.wait_ge(s_cps, u + 1)
                            act.wait_ge(s_term, u + 1)
                            act.activation(c_row[k].rearrange("p (h t) -> p h t", h=HALVES), bank[:, 4:6, :],
                                           ACT.Copy).then_inc(s_crow, 1)

            act.wait_ge(s_small, SMALL)
            act.wait_ge(s_const, NCONST)
            ffn(0)
            mixer()
            ffn(1)

        @block.vector
        def _(dve):
            for s in (s_cent, s_xn, s_prod, s_hid, s_xadd, s_bl, s_dl, s_scan, s_skip, s_xmix):
                dve.sem_inc(s, CREDIT[s])

            def norm(blk, n, dst, r=None):
                xb = x[:, ds(blk * BLK, BLK)]
                dve.wait_ge(s_xn, n + 1)
                dve.wait_ge(s_mean, n + 1)
                dve.tensor_tensor(cent[:, :], xb, bank[:, 0, :], ALU.subtract).then_inc(s_cent, 1)
                dve.wait_ge(s_rstd, n + 1)
                if r is not None:
                    dve.wait_ge(s_xlo, r + 1)
                dve.tensor_tensor(dst, cent[:, :], sq[:, :], ALU.mult).then_inc(s_xn, 1)

            CHAIN = 27

            def route(r):
                done = [0]

                def chain(ins):
                    done[0] += 1
                    ins.then_inc(s_vec, 1)
                    dve.wait_ge(s_vec, r * CHAIN + done[0])

                def tt(o, a, b, op):
                    chain(dve.tensor_tensor(o, a, b, op))

                dve.wait_ge(s_expo, r + 1)
                chain(dve.tensor_scalar(expo[:, :], expo[:, :], 1.0, None, ALU.add))
                chain(dve.reciprocal(score[:, :], expo[:, :]))
                c3 = choice[:, :].rearrange("p (t e) -> p t e", t=SUB)
                tt(c3, score[:, :].rearrange("p (t e) -> p t e", t=SUB),
                   gate_b_sb[:, :].unsqueeze(1).broadcast_to([P, SUB, EXPERTS]), ALU.add)
                cg = choice[:, :].rearrange("p (g e) -> p g e", g=NG)
                h4 = hi4[:, :].rearrange("p (g e) -> p g e", g=NG)
                l4 = lo4[:, :].rearrange("p (g e) -> p g e", g=NG)
                n2 = mn[:, :].rearrange("p (g e) -> p g e", g=NG)
                m2 = ml[:, :].rearrange("p (g e) -> p g e", g=NG)
                tt(h4, cg[:, :, 0:4], cg[:, :, 4:8], ALU.max)
                tt(l4, cg[:, :, 0:4], cg[:, :, 4:8], ALU.min)
                for w in (2, 1):
                    tt(n2[:, :, 0:w], h4[:, :, 0:w], h4[:, :, w:2 * w], ALU.min)
                    tt(m2[:, :, 0:w], l4[:, :, 0:w], l4[:, :, w:2 * w], ALU.max)
                    tt(h4[:, :, 0:w], h4[:, :, 0:w], h4[:, :, w:2 * w], ALU.max)
                    tt(l4[:, :, 0:w], n2[:, :, 0:w], m2[:, :, 0:w], ALU.max)
                tt(gscore[:, :, 0:GROUPS], h4[:, :, 0].rearrange("p (t g) -> p t g", t=SUB),
                   l4[:, :, 0].rearrange("p (t g) -> p t g", t=SUB), ALU.add)
                dve.sem_inc(s_pass, 1)
                for t in range(SUB):
                    i = dve.max(top8[:, 0, t, :], gscore[:, t, :])
                chain(i)
                dve.sem_inc(s_pass, 1)
                for t in range(SUB):
                    i = dve.match_replace(gleft[:, t, :], top8[:, 0, t, :], gscore[:, t, :], GONE)
                chain(i)
                tt(gmask[:, :].rearrange("p (t g) -> p t g", t=SUB), gscore[:, :, 0:GROUPS],
                   gleft[:, :, 0:GROUPS], ALU.not_equal)
                tt(cg, cg, gmask[:, :].unsqueeze(2).broadcast_to([P, NG, PER_GROUP]), ALU.mult)
                dve.sem_inc(s_pass, 1)
                for t in range(SUB):
                    i = dve.max(top8[:, 1, t, :], choice[:, t * EXPERTS:(t + 1) * EXPERTS])
                chain(i)
                dve.sem_inc(s_pass, 1)
                for t in range(SUB):
                    at = slice(t * EXPERTS, (t + 1) * EXPERTS)
                    i = dve.match_replace(rest[:, at], top8[:, 1, t, :], choice[:, at], GONE)
                chain(i)
                tt(rest[:, :], rest[:, :], choice[:, :], ALU.not_equal)
                tt(score[:, :], score[:, :], rest[:, :], ALU.mult)
                s3 = score[:, :].rearrange("p (t e) -> p t e", t=SUB)
                chain(dve.tensor_reduce(denom[:, :], s3, AX_X, ALU.add))
                chain(dve.tensor_scalar(denom[:, :], denom[:, :], 1e-20, 1.0 / (ROUTED_SCALE * WS), ALU.add, ALU.mult))
                chain(dve.reciprocal(denom[:, :], denom[:, :]))
                tt(s3, s3, denom[:, :].unsqueeze(2).broadcast_to([P, SUB, EXPERTS]), ALU.mult)
                chain(dve.tensor_copy(rwp[:, :, 0:EXPERTS], s3))
                assert done[0] == CHAIN, done[0]
                dve.tensor_tensor(rwp[:, :, EXPERTS:], s3, rwp[:, :, 0:EXPERTS], ALU.subtract).then_inc(s_rwp, 1)

            def hidden(u, k, rw=None):
                dve.wait_ge(s_silu, done(s_silu, u))
                dve.wait_ge(s_u, u + 1)
                dve.scalar_tensor_tensor(prod[k], bank[:, 2 + k, :], 1.0 / WS, silu_g[k], ALU.mult, ALU.mult)\
                    .then_inc(s_prod, 1)
                dve.wait_ge(s_prod, done(s_prod, u))
                dve.wait_ge(s_hlo, u + 1)
                if rw is not None:
                    dve.wait_ge(s_rw, rw + 1)
                    dve.tensor_tensor(hid[k], prod[k], bank[:, 4 + k, :], ALU.mult).then_inc(s_hid, 1)
                else:
                    dve.tensor_scalar(hid[k], prod[k], WS, None, ALU.mult).then_inc(s_hid, 1)

            def ffn(layer):
                with dve.Fori(0, NBLK) as blk:
                    norm(blk, 2 * layer * NBLK + blk, xn[:, :], layer * NBLK + blk)
                    route(layer * NBLK + blk)
                if layer == 0:
                    for c, (w, at, n, src, rows) in enumerate(chunks):
                        dve.wait_ge(s_whi, c + 1)
                        dve.scalar_tensor_tensor(w[1][0:rows, at:at + n], stage(c), WS, w[0][0:rows, at:at + n],
                                                 ALU.mult, ALU.subtract).then_inc(s_split, 1)
                base, rbase = layer * NBLK * TILES, layer * NBLK * ROUTED_TILES

                def tiles(blk, last=False):
                    u, r = base + blk * TILES, rbase + blk * ROUTED_TILES
                    with dve.Fori(1, ROUTED_TILES // 2) as p:
                        for k in range(2):
                            hidden(u + 2 * p + k, k, r + 2 * p + k)
                    for j in range(ROUTED_TILES, TILES):
                        hidden(u + j, j % 2)
                    if not last:
                        for k in range(2):
                            hidden(u + TILES + k, k, r + ROUTED_TILES + k)
                    dve.wait_ge(s_dn, done(s_dn, u + TILES - 1))
                    xb = x[:, ds(blk * BLK, BLK)]
                    dve.scalar_tensor_tensor(xb, bank[:, 6, :], 0.5 / (WS * WS), xb, ALU.mult, ALU.add)\
                        .then_inc(s_xadd, 1)
                for k in range(2):
                    hidden(base + k, k, rbase + k)
                with dve.Fori(0, NBLK - 1) as blk:
                    tiles(blk)
                tiles(NBLK - 1, last=True)

            def mixer():
                dve.wait_ge(s_aneg, 1)
                dve.tensor_scalar(a_neg[:, :], a_neg[:, :], -1.0, None, ALU.mult).then_inc(s_aneg, 1)
                lp = left[:, :].rearrange("p (b t) -> p b t", b=BATCH)
                dve.memset(lp[:, :, 0:TAPS - 1], 0.0).then_inc(s_pad, 1)
                with dve.Fori(0, NBLK) as blk:
                    norm(blk, NBLK + blk, normed[:, ds(blk * BLK, BLK)])
                dve.wait_ge(s_pad, 1)
                with dve.Fori(0, BATCH) as b:
                    tap = [left[:, ds(b * (SEQ + TAPS - 1) + k, SEQ)] for k in range(TAPS)]
                    w = [vecs[:, V_TAP + k:V_TAP + k + 1] for k in range(TAPS)]
                    dve.wait_ge(s_lsb, done(s_lsb, b * HALVES + HALVES - 1))
                    dve.tensor_scalar(term[0], tap[0], w[0], None, ALU.mult).then_inc(s_taps, 1)
                    dve.wait_ge(s_taps, 2 * b + 1)
                    dve.scalar_tensor_tensor(term[1], tap[1], w[1], term[0], ALU.mult, ALU.add).then_inc(s_taps, 1)
                    dve.wait_ge(s_taps, 2 * b + 2)
                    dve.wait_ge(s_x1, b + 1)
                    dve.scalar_tensor_tensor(state[0], tap[2], w[2], term[1], ALU.mult, ALU.add).then_inc(s_conv, 1)
                with dve.Fori(0, BATCH) as b:
                    for h in range(HALVES):
                        n = b * HALVES + h
                        at = b * SEQ + h * BLK
                        dve.wait_ge(s_rel, done(s_rel, n))
                        dve.tensor_tensor(delta[:, ds(at, BLK)], decay[0][:, 0:BLK], decay[1][:, 0:BLK], ALU.add)\
                            .then_inc(s_dl, 1)
                        dve.wait_ge(s_dl, done(s_dl, n))
                        dve.tensor_tensor(dx[:, ds(at, BLK)], delta[:, ds(at, BLK)], conv_x[:, ds(at, BLK)], ALU.mult)\
                            .then_inc(s_dxs, 1)
                        low = slice(STATE, P)
                        for dst, hi_done, bk, v in ((bs, s_bh, 2, V_B), (cs, s_ch, 4, V_C)):
                            part = dst[low, ds(at, BLK)]
                            dve.wait_ge(hi_done, n + 1)
                            dve.scalar_tensor_tensor(part, bank[low, bk + h, :], vecs[low, v:v + 1], part,
                                                     ALU.add, ALU.subtract).then_inc(s_bl, 1)
                dve.wait_ge(s_dxs, NBLK)
                with dve.Fori(0, BATCH) as b:
                    with dve.Fori(0, STATE // 2) as p:
                        for k in range(2):
                            u = b * STATE + 2 * p + k
                            dbx = bank[:, 2 * k:2 * k + 2, :]
                            dve.wait_ge(s_bps, u + 1)
                            dve.tensor_tensor(dbx, dbx, dx[:, ds(b * SEQ, SEQ)].rearrange("p (h t) -> p h t", h=HALVES),
                                              ALU.mult).then_inc(s_dbx, 1)
                        for k in range(2):
                            u = b * STATE + 2 * p + k
                            dve.wait_ge(s_dbx, u + 1)
                            dve.wait_ge(s_dec, u + 1)
                            dve.wait_ge(s_term, u + 1)
                            dve.tensor_tensor_scan(state[k], decay[k],
                                                   bank[:, 2 * k:2 * k + 2, :].rearrange("p h t -> p (h t)"),
                                                   0.0, ALU.mult, ALU.add).then_inc(s_scan, 1)
                    at = b * SEQ
                    split = lambda ap: ap.rearrange("p (h t) -> p h t", h=HALVES)
                    dve.wait_ge(s_yacc, done(s_yacc, b * STATE + STATE - 1))
                    dve.scalar_tensor_tensor(split(delta[:, ds(at, SEQ)]), split(conv_x[:, ds(at, SEQ)]),
                                             vecs[:, V_SKIP:V_SKIP + 1], bank[:, 6:8, :], ALU.mult, ALU.add)\
                        .then_inc(s_skip, 1)
                    dve.wait_ge(s_skip, done(s_skip, b))
                    dve.tensor_tensor(gate[:, ds(at, SEQ)], gate[:, ds(at, SEQ)], delta[:, ds(at, SEQ)], ALU.mult)\
                        .then_inc(s_gated, 1)
                with dve.Fori(0, BATCH) as b:
                    for h in range(HALVES):
                        n = b * HALVES + h
                        xb = x[:, ds(b * SEQ + h * BLK, BLK)]
                        dve.wait_ge(s_mix, n + 1)
                        dve.scalar_tensor_tensor(xb, bank[:, h, :], vecs[:, V_DOWN:V_DOWN + 1], xb, ALU.add, ALU.add)\
                            .then_inc(s_xmix, 1)

            dve.wait_ge(s_x, 64)
            dve.wait_ge(s_small, SMALL)
            dve.wait_ge(s_const, NCONST)
            ffn(0)
            mixer()
            ffn(1)

        @block.gpsimd
        def _(pool):
            pool.sem_inc(s_xlo, CREDIT[s_xlo])
            pool.sem_inc(s_hlo, CREDIT[s_hlo])
            pool.sem_inc(s_term, CREDIT[s_term])
            pool.memset(mean_w[:, :], 1.0 / P).then_inc(s_const, 1)
            pool.memset(eps_col[:, :], EPS).then_inc(s_const, 1)
            pool.memset(gscore[:, :, GROUPS:], PAD).then_inc(s_const, 1)
            for w in wg + wu:
                pool.memset(w[:, ROWS:], 0.0).then_inc(s_const, 1)
            for w in wd:
                pool.memset(w[:, (TILES - 1) * P:], 0.0).then_inc(s_const, 1)

            def ffn(layer):
                with pool.Fori(0, NBLK) as blk:
                    pool.wait_ge(s_xhi, layer * NBLK + blk + 1)
                    pool.tensor_tensor(xh[:, ds(blk * BLK + TOKENS, BLK)], xn[:, :], xh[:, ds(blk * BLK, BLK)],
                                       ALU.subtract).then_inc(s_xlo, 1)
                base = layer * NBLK * TILES
                with pool.Fori(0, NBLK * TILES // 2) as p:
                    for k in range(2):
                        u = base + 2 * p + k
                        pool.wait_ge(s_hhi, u + 1)
                        pool.tensor_tensor(hid_lo[k], hid[k], hid_hi[k], ALU.subtract).then_inc(s_hlo, 1)

            ffn(0)
            with pool.Fori(0, BATCH * STATE // 2) as p:
                for k in range(2):
                    u = 2 * p + k
                    pool.wait_ge(s_scan, done(s_scan, u))
                    pool.wait_ge(s_crow, done(s_crow, u))
                    pool.wait_ge(s_yacc, u + 1)
                    pool.tensor_tensor(term[k], state[k], c_row[k], ALU.mult).then_inc(s_term, 1)
            ffn(1)


_OUT = (P, TOKENS)


def kernel(**inputs):
    import numpy as np
    import concourse.bacc as bacc
    from concourse.bass_utils import run_bass_kernel_spmd as run

    a = {k.split("_", 2)[2]: np.asarray(v) for k, v in inputs.items()}
    rows = lambda w: w.reshape(-1, w.shape[-1])
    h = P
    col = lambda v: v.reshape(P, 1)
    twice = lambda v: np.concatenate([v, v], axis=-1)
    wd_rows = np.concatenate([a["Wd"].transpose(0, 2, 1).reshape(-1, h), a["Sd"].T], axis=0)
    full = (TILES - 1) * P
    expert_of_row = np.arange(ROUTED_ROWS) // INNER
    row_of_expert = (expert_of_row[None, :] == np.arange(EXPERTS)[:, None]).astype(np.float16)
    one_hot = np.eye(STATE, dtype=np.float16)
    arrays = {
        "x_in": a["up_x"].reshape(TOKENS, P).T,
        "w_up": a["W_up"],
        "w_delta": a["W_delta"],
        "w_b2": twice(a["W_B"]),
        "w_c2": twice(a["W_C"]),
        "w_down": a["W_down"],
        "vecs_in": np.concatenate([col(a["b_up"][:P]), col(a["b_up"][P:]), a["conv_w"], col(a["conv_b"]),
                                   col(a["b_delta"]), col(twice(a["b_B"])), col(twice(a["b_C"])),
                                   col(a["D_skip"]), col(a["b_down"])], axis=1),
        "a_log": a["A_log"],
        "gate_wt": a["gate_w"].T,
        "gate_bias": np.broadcast_to(a["gate_bias"], (P, EXPERTS)),
        "wg_in": np.concatenate([rows(a["Wg"]), a["Sg"]], axis=0).T,
        "wu_in": np.concatenate([rows(a["Wu"]), a["Su"]], axis=0).T,
        "wd_in": wd_rows[:full].reshape(TILES - 1, P, h).transpose(1, 0, 2).reshape(P, full),
        "wd_last": wd_rows[full:],
        "row_of_expert_in": np.concatenate([row_of_expert, row_of_expert], axis=0),
        "one_hot_in": np.concatenate([one_hot, one_hot], axis=0),
        "eye_in": np.eye(P, dtype=np.float32),
        "eye16_in": np.eye(P, dtype=np.float16),
    }
    arrays = {k: np.ascontiguousarray(v) for k, v in arrays.items()}
    nc = bacc.Bacc("TRN2", target_bir_lowering=False, num_devices=1)
    args = [nc.dram_tensor(k, v.shape, mybir.dt.from_np(v.dtype), kind="ExternalInput").ap()
            for k, v in arrays.items()]
    args.append(nc.dram_tensor("out", _OUT, F32, kind="ExternalOutput").ap())
    macaron(nc, *args)
    got = run(nc, [arrays], core_ids=[0]).results[0]["out"]
    return np.ascontiguousarray(got.T).reshape(BATCH, SEQ, P)
```

```python
from contextlib import ExitStack

import concourse.bass as bass
from concourse import mybir

F32 = mybir.dt.float32
F16 = mybir.dt.float16
ALU = mybir.AluOpType
ACT = mybir.ActivationFunctionType
AX_X = mybir.AxisListType.X
ds = bass.ds

P = 128
BATCH, SEQ = 4, 1024
TOKENS = BATCH * SEQ
BLK = 512
NBLK = TOKENS // BLK
HALVES = SEQ // BLK
SUB = BLK // P
HSLOTS = 4
HLAG = 3
PREP = 20
MAGIC = 0x5F3759DF
NEWTON = 3
SLOTS = 4
YLAG = 3
STATE = 64
TAPS = 3
EXPERTS, INNER, SHARED = 64, 88, 176
GROUPS, KEEP_GROUPS, TOPK = 8, 4, 8
PER_GROUP = EXPERTS // GROUPS
ROUTED_ROWS = EXPERTS * INNER
ROWS = ROUTED_ROWS + SHARED
ROUTED_TILES = ROUTED_ROWS // P
TILES = -(-ROWS // P)
LAST = ROWS - (TILES - 1) * P
ROUTED_SCALE = 2.5
EPS = 1e-5
WS = 64.0
PAD = 1e30
GONE = -1e30
GPAD = GROUPS + KEEP_GROUPS

V_UPL, V_UPR, V_TAP, V_CONV, V_DELTA, V_B, V_C, V_SKIP, V_DOWN = 0, 1, 2, 5, 6, 7, 8, 9, 10
NVEC = 11


def macaron(nc, x_in, w_up, w_delta, w_b2, w_c2, w_down, vecs_in, a_log, gate_wt, gate_bias,
            wg_in, wu_in, wd_in, wd_last, row_of_expert_in, one_hot_in, eye_in, eye16_in, out):
    ctx = ExitStack()
    with ctx:
        def sb(name, shape, dt=F32):
            return ctx.enter_context(nc.sbuf_tensor(name, shape, dt))

        def sem(name):
            return ctx.enter_context(nc.semaphore(name))

        x = sb("x", [P, TOKENS])
        wg = [sb(f"wg_{k}", [P, TILES * P], F16) for k in ("high", "low")]
        wu = [sb(f"wu_{k}", [P, TILES * P], F16) for k in ("high", "low")]
        wd = [sb(f"wd_{k}", [P, TILES * P], F16) for k in ("high", "low")]
        row_of_expert = sb("row_of_expert", [P, P], F16)
        F1 = sb("F1", [P, TOKENS])
        F2 = sb("F2", [P, BATCH * (SEQ + TAPS - 1)])
        F3 = sb("F3", [P, TOKENS])
        F4 = sb("F4", [P, TOKENS])
        xh = F1[:, :].bitcast(F16)
        rwt = F2[:, :].bitcast(F16)
        delta = F1
        left, dx = F2, F2
        normed, conv_x = F3, F3
        gate = F4
        bs = sb("b_halves", [P, TOKENS], F16)
        cs = sb("c_halves", [P, TOKENS], F16)
        arena = sb("arena", [P, (4 + SLOTS) * SEQ])
        silu_g = [arena[:, k * BLK:(k + 1) * BLK] for k in range(2)]
        prod = [arena[:, (2 + k) * BLK:(3 + k) * BLK] for k in range(2)]
        hid = [arena[:, (4 + k) * BLK:(5 + k) * BLK] for k in range(2)]
        halves = arena[:, 6 * BLK:(6 + HSLOTS + TILES - ROUTED_TILES) * BLK].bitcast(F16)
        hid_hi = [halves[:, 2 * k * BLK:(2 * k + 1) * BLK] for k in range(HSLOTS + TILES - ROUTED_TILES)]
        hid_lo = [halves[:, (2 * k + 1) * BLK:(2 * k + 2) * BLK] for k in range(HSLOTS + TILES - ROUTED_TILES)]
        decay = [arena[:, k * SEQ:(k + 1) * SEQ] for k in range(2)]
        state = [arena[:, (2 + k) * SEQ:(3 + k) * SEQ] for k in range(2)]
        term = [arena[:, (4 + k) * SEQ:(5 + k) * SEQ] for k in range(SLOTS)]

        w_up_sb = sb("w_up_sb", [P, 2 * P])
        w_delta_sb = sb("w_delta_sb", [P, P])
        w_b_sb = sb("w_b_sb", [P, P])
        w_c_sb = sb("w_c_sb", [P, P])
        w_down_sb = sb("w_down_sb", [P, P])
        vecs = sb("vecs", [P, NVEC])
        a_neg = sb("a_neg", [P, STATE])
        gate_w_sb = sb("gate_w_sb", [P, EXPERTS])
        gate_b_sb = sb("gate_b_sb", [P, EXPERTS])
        one_hot = sb("one_hot", [P, STATE], F16)
        eye = sb("eye", [P, P])
        eye16 = sb("eye16", [P, P], F16)
        mean_w = sb("mean_w", [P, P])

        NE = SUB * EXPERTS
        NG = SUB * GROUPS
        cf, bf = cs[:, :].bitcast(F32), bs[:, :].bitcast(F32)
        cent, sq, xn = [cf[:, k * BLK:(k + 1) * BLK] for k in range(3)]
        sqs = [cf[:, k * BLK:(k + 1) * BLK] for k in range(2)]
        expo, score, choice, rest = [bf[:, k * NE:(k + 1) * NE] for k in range(4)]
        hi4, lo4 = [bf[:, (4 * NE + k * NG * 4):(4 * NE + (k + 1) * NG * 4)] for k in range(2)]
        mn, ml = [bf[:, (5 * NE + k * NG * 2):(5 * NE + (k + 1) * NG * 2)] for k in range(2)]
        rwp = bs[:, 12 * NE:14 * NE].rearrange("p (t e) -> p t e", t=SUB)
        top8 = sb("top8", [P, 2, SUB, 8])
        gscore = sb("gscore", [P, SUB, GPAD])
        gleft = sb("gleft", [P, SUB, GPAD])
        gmask = sb("gmask", [P, NG])
        denom = sb("denom", [P, SUB])
        nt = NBLK * SUB
        var_t, tmp_t, rstd_t = [sb(f"rstd_{k}", [P, nt]) for k in range(3)]

        bank = ctx.enter_context(nc.psum_tensor("bank", [P, 8, BLK], F32))

        s_x = sem("x_loaded")
        s_small = sem("small_loaded")
        s_stage = [sem(f"stage_loaded{k}") for k in range(4)]
        s_split = sem("weights_split")
        s_const = sem("constants_set")
        s_aneg = sem("a_neg_ready")
        s_out = sem("out_stored")
        s_mean, s_cent, s_sq, s_var, s_rstd, s_rstd_ps, s_xn = map(sem, (
            "mean_ready", "centred", "squared", "var_ready", "rstd_ready", "rstd_spread", "normed"))
        m_mean, m_cent, m_sq, m_var, m_newton, m_rstd, m_rstd_ps, m_norm = map(sem, (
            "m_mean_ready", "m_centred", "m_squared", "m_var_ready", "m_newton_chain", "m_rstd_ready",
            "m_rstd_spread", "m_normed"))
        s_xhi, s_xlo = sem("x_high"), sem("x_low")
        s_logit, s_expo, s_rwp, s_rwt_ps, s_rwt = map(sem, (
            "logits_ready", "exp_ready", "routing_ready", "routing_transposed", "routing_stored"))
        s_vec = sem("vector_chain")
        s_g, s_u, s_rw, s_silu, s_prod, s_hid, s_hhi, s_hlo, s_dn, s_xadd = map(sem, (
            "gate_rows", "up_rows", "weight_rows", "silu_ready", "product_ready", "hidden_ready",
            "hidden_high", "hidden_low", "down_done", "x_updated"))
        s_l, s_r, s_lsb, s_gate, s_conv, s_x1, s_zd, s_zb, s_zc, s_abs, s_e, s_sp, s_rel, s_dl, s_dxs, \
            s_bh, s_ch, s_bl = map(sem, (
                "left_rows", "right_rows", "left_stored", "gate_stored", "conv_ready", "conv_x_ready",
                "delta_rows", "b_rows", "c_rows", "abs_ready", "exp_abs_ready", "log1p_ready", "relu_ready",
                "delta_ready", "dx_ready", "b_high", "c_high", "bc_low"))
        s_taps = sem("conv_chain")
        s_pad = sem("left_padded")
        s_bps, s_cps, s_dec, s_crow, s_dbx, s_scan, s_term, s_yacc, s_skip, s_gated = map(sem, (
            "b_spread", "c_spread", "decay_ready", "c_copied", "dbx_ready", "scan_done", "term_ready",
            "term_added", "y_skip", "gated_ready"))
        s_mix, s_xmix = sem("mixer_rows"), sem("x_mixed")

        s_pass = sem("passed")
        s_whi = sem("weight_highs_made")
        CREDIT = {s_cent: 1, s_silu: 2, s_prod: 2, s_hid: 2, s_hlo: 2, s_dn: HSLOTS, s_xadd: 1, s_xlo: 1,
                  s_lsb: 2, s_gate: 2, s_rel: 2, s_bl: 4, s_dl: 1, s_scan: 2, s_crow: 1, s_term: 2,
                  s_yacc: SLOTS, s_skip: 1, s_xmix: 2, s_x1: 1, s_vec: 1, m_cent: 2, m_var: 2, m_norm: 2}

        def done(s, i):
            return CREDIT[s] + i + 1

        chunks = []
        for w, src, n in ((wg, wg_in, ROWS // 3), (wu, wu_in, ROWS // 3), (wd, wd_in, (TILES - 1) * P // 3)):
            for c in range(3):
                chunks.append((w, c * n, n, src[:, c * n:(c + 1) * n], P))
        chunks.append((wd, (TILES - 1) * P, P, wd_last, LAST))
        stage_of = [(F3, 0), (F3, 2048), (F4, 0), (F4, 2048)]

        def stage(c):
            buf, at = stage_of[c % 4]
            return buf[0:chunks[c][4], at:at + chunks[c][2]]

        AT_MEAN, AT_CENT, AT_SQUARE, AT_VAR, AT_NEWTON, AT_SPREAD, AT_NORM, AT_LOGITS, AT_TANH, AT_ROUTE = \
            0, 1, 1, 2, 3, 6, 7, 8, 8, 9

        block = ctx.enter_context(nc.Block())

        @block.sync
        def _(sp):
            for k in range(4):
                w = TOKENS // 4
                sp.dma_start(x[:, k * w:(k + 1) * w], x_in[:, k * w:(k + 1) * w]).then_inc(s_x, 16)
            for dst, src in ((gate_w_sb, gate_wt), (gate_b_sb, gate_bias), (eye16, eye16_in), (vecs, vecs_in),
                             (a_neg, a_log), (w_up_sb, w_up), (w_delta_sb, w_delta), (w_b_sb, w_b2),
                             (w_c_sb, w_c2), (w_down_sb, w_down), (one_hot, one_hot_in), (eye, eye_in), (row_of_expert, row_of_expert_in)):
                sp.dma_start(dst[:, :], src).then_inc(s_small, 16)
            for c, (w, at, n, src, rows) in enumerate(chunks):
                if c >= 4:
                    sp.wait_ge(s_split, c - 4 + 1)
                sp.dma_start(stage(c), src).then_inc(s_stage[c % 4], 16)
            with sp.Fori(0, NBLK) as blk:
                sp.wait_ge(s_xadd, done(s_xadd, NBLK + blk))
                sp.dma_start(out[:, ds(blk * BLK, BLK)], x[:, ds(blk * BLK, BLK)]).then_inc(s_out, 16)
            sp.wait_ge(s_out, 16 * NBLK)

        SMALL = 16 * 13
        NCONST = 8

        @block.tensor
        def _(pe):
            for s in (s_dn, s_yacc, m_var):
                pe.sem_inc(s, CREDIT[s])

            def mm(dst, lhsT, rhs, start=True, stop=True):
                return pe.matmul(dst, lhsT, rhs, start=start, stop=stop)

            def column_of_rstd(t):
                return rstd_t[:, t:t + 1].broadcast_to([P, P])

            def prepare(place, blk, r):
                if place == AT_MEAN:
                    mm(bank[:, 7, :], mean_w[:, :], x[:, ds(blk * BLK, BLK)]).then_inc(s_mean, 1)
                if place == AT_VAR:
                    pe.wait_ge(s_sq, r + 1)
                    for t in range(SUB):
                        i = mm(bank[:, 7, t:t + 1], sq[:, t * P:(t + 1) * P], mean_w[:, 0:1])
                    i.then_inc(s_var, 1)
                if place == AT_SPREAD:
                    pe.wait_ge(s_rstd, r + 1)
                    for t in range(SUB):
                        i = mm(bank[:, 7, t * P:(t + 1) * P], column_of_rstd(t), eye[:, :])
                    i.then_inc(s_rstd_ps, 1)
                if place == AT_LOGITS:
                    pe.wait_ge(s_xn, r + 1)
                    for t in range(SUB):
                        i = mm(bank[:, 7, t * EXPERTS:(t + 1) * EXPERTS], xn[:, t * P:(t + 1) * P], gate_w_sb[:, :])
                    i.then_inc(s_logit, 1)
                if place == PREP:
                    pe.wait_ge(s_rwp, r + 1)
                    dst = bank[:, 7, 0:BLK // 2].bitcast(F16)
                    for t in range(SUB):
                        i = pe.transpose(dst[:, t * P:(t + 1) * P], rwp[:, t, :], eye16[:, :])
                    i.then_inc(s_rwt_ps, 1)

            def weight_rows(blk, n):
                pe.wait_ge(s_rwt, n + 1)
                if not (isinstance(n, int) and n == 0):
                    pe.wait_ge(s_hid, done(s_hid, n * TILES - (TILES - ROUTED_TILES) - 1))
                mm(bank[:, 4, :], row_of_expert[:, :], rwt[:, ds(blk * BLK, BLK)]).then_inc(s_rw, 1)

            def rows(blk, j, u, k):
                hi, lo = xh[:, ds(blk * BLK, BLK)], xh[:, ds(blk * BLK + TOKENS, BLK)]

                def product(dst, w):
                    wh, wl = w[0][:, ds(j * P, P)], w[1][:, ds(j * P, P)]
                    mm(dst, wh, hi, True, False)
                    mm(dst, wh, lo, False, False)
                    return mm(dst, wl, hi, False, True)
                pe.wait_ge(s_silu, u + 1)
                product(bank[:, k, :], wg).then_inc(s_g, 1)
                pe.wait_ge(s_prod, u + 1)
                product(bank[:, 2 + k, :], wu).then_inc(s_u, 1)
            def down(j, u, slot, start=False, stop=False):
                pe.wait_ge(s_hlo, done(s_hlo, u))
                wh, wl = wd[0][:, ds(j * P, P)], wd[1][:, ds(j * P, P)]
                mm(bank[:, 6, :], wh, hid_hi[slot], start, False)
                mm(bank[:, 6, :], wh, hid_lo[slot], False, False)
                mm(bank[:, 6, :], wl, hid_hi[slot], False, stop).then_inc(s_dn, 1)

            def ffn(layer):
                for place in range(PREP + 1):
                    prepare(place, 0, layer * NBLK)
                if layer == 0:
                    pe.wait_ge(s_split, len(chunks))
                base = layer * NBLK * TILES

                def tiles(blk, last=False):
                    u = base + blk * TILES

                    def step(q, j, k, start=False):
                        rows(blk, q + j, u + q + j, j % 2)
                        d = q + j - HLAG
                        if start:
                            pe.wait_ge(s_xadd, layer * NBLK + blk + 1)
                        down(d, u + d, (k - HLAG) % HSLOTS, start=start)

                    step(0, HLAG, HLAG, start=True)
                    for place in range(PREP):
                        step(0, HSLOTS + place, place)
                        if not last:
                            prepare(place, blk + 1, layer * NBLK + blk + 1)
                    with pe.Fori(1 + PREP // HSLOTS, ROUTED_TILES // HSLOTS) as q:
                        for k in range(HSLOTS):
                            step(HSLOTS * q, k, k)
                    if not last:
                        prepare(PREP, blk + 1, layer * NBLK + blk + 1)
                    for j in range(ROUTED_TILES, TILES):
                        step(0, j, j)
                    for k in range(HLAG):
                        if not last:
                            if k == 0:
                                weight_rows(blk + 1, layer * NBLK + blk + 1)
                                pe.wait_ge(s_xlo, done(s_xlo, layer * NBLK + blk + 1))
                            rows(blk + 1, k, u + TILES + k, k % 2)
                        j = TILES - HLAG + k
                        down(j, u + j, j % HSLOTS if j < ROUTED_TILES else HSLOTS + j - ROUTED_TILES,
                             stop=(k == HLAG - 1))
                weight_rows(0, layer * NBLK)
                pe.wait_ge(s_xlo, done(s_xlo, layer * NBLK))
                for k in range(HLAG):
                    rows(0, k, base + k, k % 2)
                with pe.Fori(0, NBLK - 1) as blk:
                    tiles(blk)
                tiles(NBLK - 1, last=True)

            def mixer():
                def variance(n, k):
                    pe.wait_ge(m_sq, n + 1)
                    for t in range(SUB):
                        i = mm(bank[:, 2, ds(n * SUB + t, 1)], sqs[k][:, t * P:(t + 1) * P], mean_w[:, 0:1])
                    i.then_inc(m_var, 1)

                for k in range(2):
                    mm(bank[:, k, :], mean_w[:, :], x[:, k * BLK:(k + 1) * BLK]).then_inc(m_mean, 1)
                with pe.Fori(0, NBLK // 2 - 1) as n:
                    for k in range(2):
                        variance(2 * n + k, k)
                        pe.wait_ge(m_cent, 2 * n + k + 3)
                        mm(bank[:, k, :], mean_w[:, :], x[:, ds((2 * n + k + 2) * BLK, BLK)]).then_inc(m_mean, 1)
                for k in range(2):
                    variance(NBLK - 2 + k, k)
                pe.wait_ge(m_rstd, 1)
                for n in range(NBLK):
                    pe.wait_ge(m_norm, n + 1)
                    for t in range(SUB):
                        i = mm(bank[:, 4 + n % 2, t * P:(t + 1) * P], column_of_rstd(n * SUB + t), eye[:, :])
                    i.then_inc(m_rstd_ps, 1)
                pe.wait_ge(m_norm, done(m_norm, NBLK - 1))
                with pe.Fori(0, BATCH) as b:
                    for h in range(HALVES):
                        n = b * HALVES + h
                        src = normed[:, ds(b * SEQ + h * BLK, BLK)]
                        pe.wait_ge(s_lsb, n + 1)
                        mm(bank[:, h, :], w_up_sb[:, 0:P], src).then_inc(s_l, 1)
                        pe.wait_ge(s_gate, n + 1)
                        mm(bank[:, 2 + h, :], w_up_sb[:, P:2 * P], src).then_inc(s_r, 1)
                pe.wait_ge(s_lsb, done(s_lsb, NBLK - 1))
                pe.wait_ge(s_gate, done(s_gate, NBLK - 1))
                with pe.Fori(0, BATCH) as b:
                    for h in range(HALVES):
                        n = b * HALVES + h
                        src = conv_x[:, ds(b * SEQ + h * BLK, BLK)]
                        pe.wait_ge(s_x1, done(s_x1, b))
                        pe.wait_ge(s_rel, n + 1)
                        mm(bank[:, h, :], w_delta_sb[:, :], src).then_inc(s_zd, 1)
                        pe.wait_ge(s_bl, 2 * n + 1)
                        mm(bank[:, 2 + h, :], w_b_sb[:, :], src).then_inc(s_zb, 1)
                        pe.wait_ge(s_bl, 2 * n + 2)
                        mm(bank[:, 4 + h, :], w_c_sb[:, :], src).then_inc(s_zc, 1)

                pe.wait_ge(s_bl, done(s_bl, 2 * NBLK - 1))
                pe.wait_ge(s_rel, done(s_rel, NBLK - 1))

                def pair(b, n, adds):
                    halves = [(h, *add) for add in adds for h in range(HALVES)]

                    def add_half():
                        if not halves:
                            return
                        h, base, j, start, stop = halves.pop(0)
                        if h == 0:
                            if start:
                                pe.wait_ge(s_skip, b + 1)
                            pe.wait_ge(s_term, done(s_term, base + j))
                        i = mm(bank[:, 6 + h, :], eye[:, :], term[j % SLOTS][:, h * BLK:(h + 1) * BLK], start, stop)
                        if h == HALVES - 1:
                            i.then_inc(s_yacc, 1)

                    if n is None:
                        while halves:
                            add_half()
                        return
                    for stack, first, freed, ready in ((bs, 0, s_scan, s_bps), (cs, 4, s_crow, s_cps)):
                        for k in range(2):
                            at = n[0] + n[1] + k
                            sel = one_hot[:, ds(at, 1)].broadcast_to([P, P])
                            pe.wait_ge(freed, b * STATE + at + 1)
                            for h in range(HALVES):
                                to = first + h + (2 * k if stack is bs else 0)
                                i = mm(bank[:, to, :], sel, stack[:, ds(b * SEQ + h * BLK, BLK)])
                            i.then_inc(ready, 1)
                            for _ in range({(0, 0): 1, (0, 1): 0, (4, 0): 2, (4, 1): 1}[first, k]):
                                add_half()

                def states(b, first=False):
                    u = b * STATE
                    over = [] if first else [(u - STATE, STATE - YLAG + k, False, k == YLAG - 1) for k in range(YLAG)]
                    pair(b, (0, 0), over[:2])
                    pair(b, (0, 2), over[2:] + [(u, 0, True, False)])
                    with pe.Fori(1, STATE // SLOTS) as q:
                        for k in range(0, SLOTS, 2):
                            pair(b, (SLOTS * q, k), [(u + SLOTS * q, k - YLAG + j, False, False) for j in range(2)])
                states(0, first=True)
                with pe.Fori(1, BATCH) as b:
                    states(b)
                pair(BATCH, None, [((BATCH - 1) * STATE, STATE - YLAG + k, False, k == YLAG - 1) for k in range(YLAG)])
                with pe.Fori(0, BATCH) as b:
                    for h in range(HALVES):
                        pe.wait_ge(s_gated, b + 1)
                        pe.wait_ge(s_xmix, b * HALVES + h + 1)
                        mm(bank[:, h, :], w_down_sb[:, :], gate[:, ds(b * SEQ + h * BLK, BLK)]).then_inc(s_mix, 1)

            pe.wait_ge(s_x, 64)
            pe.wait_ge(s_small, SMALL)
            pe.wait_ge(s_const, NCONST)
            ffn(0)
            pe.wait_ge(s_xadd, NBLK + 1)
            mixer()
            pe.wait_ge(s_xmix, 2 + NBLK)
            ffn(1)

        @block.scalar
        def _(act):
            for s in (s_silu, s_lsb, s_gate, s_rel, s_crow, s_x1):
                act.sem_inc(s, CREDIT[s])

            def prepare(place, blk, r):
                if place == AT_SQUARE:
                    act.wait_ge(s_cent, r + 1)
                    act.activation(sq, cent, ACT.Square).then_inc(s_sq, 1)
                if place == AT_TANH:
                    act.wait_ge(s_xn, r + 1)
                    act.activation(xh[:, ds(blk * BLK, BLK)], xn, ACT.Copy).then_inc(s_xhi, 1)
                    act.wait_ge(s_logit, r + 1)
                    act.activation(expo, bank[:, 7, 0:NE], ACT.Tanh, scale=0.5).then_inc(s_expo, 1)
                if place == PREP:
                    act.wait_ge(s_rwt_ps, r + 1)
                    act.activation(rwt[:, ds(blk * BLK, BLK)], bank[:, 7, 0:BLK // 2].bitcast(F16), ACT.Copy)\
                        .then_inc(s_rwt, 1)

            def silu(u, k):
                act.wait_ge(s_g, u + 1)
                act.wait_ge(s_prod, u + 1)
                act.activation(silu_g[k], bank[:, k, :], ACT.Silu, scale=1.0 / WS).then_inc(s_silu, 1)

            def high(u, k, slot):
                act.wait_ge(s_hid, done(s_hid, u))
                act.wait_ge(s_dn, u + 1)
                act.activation(hid_hi[slot], hid[k], ACT.Copy).then_inc(s_hhi, 1)

            def ffn(layer):
                act.preload_act_table_set("silu_and_others")
                for place in range(PREP + 1):
                    prepare(place, 0, layer * NBLK)
                if layer == 0:
                    for c, (w, at, n, src, rows) in enumerate(chunks):
                        act.wait_ge(s_stage[c % 4], 16 * (c // 4 + 1))
                        act.activation(w[0][0:rows, at:at + n], stage(c), ACT.Copy, scale=WS).then_inc(s_whi, 1)
                base = layer * NBLK * TILES

                def tiles(blk, last=False):
                    u = base + blk * TILES
                    for j in range(HSLOTS + PREP):
                        silu(u + j + 1, (j + 1) % 2)
                        high(u + j, j % 2, j % HSLOTS)
                        if not last and j >= HSLOTS:
                            prepare(j - HSLOTS, blk + 1, layer * NBLK + blk + 1)
                    with act.Fori(1 + PREP // HSLOTS, ROUTED_TILES // HSLOTS) as q:
                        for k in range(HSLOTS):
                            silu(u + HSLOTS * q + k + 1, (k + 1) % 2)
                            high(u + HSLOTS * q + k, k % 2, k)
                    if not last:
                        prepare(PREP, blk + 1, layer * NBLK + blk + 1)
                    for j in range(ROUTED_TILES, TILES):
                        if not (last and j == TILES - 1):
                            silu(u + j + 1, (j + 1) % 2)
                        high(u + j, j % 2, HSLOTS + j - ROUTED_TILES)
                silu(base, 0)
                with act.Fori(0, NBLK - 1) as blk:
                    tiles(blk)
                tiles(NBLK - 1, last=True)

            def mixer():
                with act.Fori(0, NBLK // 2) as n:
                    for k in range(2):
                        act.wait_ge(m_cent, done(m_cent, 2 * n + k))
                        act.wait_ge(m_var, 2 * n + k + 1)
                        act.activation(sqs[k], normed[:, ds((2 * n + k) * BLK, BLK)], ACT.Square).then_inc(m_sq, 1)
                act.wait_ge(s_pad, 1)
                with act.Fori(0, BATCH) as b:
                    for h in range(HALVES):
                        n = b * HALVES + h
                        act.wait_ge(s_l, n + 1)
                        act.activation(left[:, ds(b * (SEQ + TAPS - 1) + TAPS - 1 + h * BLK, BLK)], bank[:, h, :],
                                       ACT.Identity, bias=vecs[:, V_UPL:V_UPL + 1]).then_inc(s_lsb, 1)
                    for h in range(HALVES):
                        n = b * HALVES + h
                        act.wait_ge(s_r, n + 1)
                        act.activation(gate[:, ds(b * SEQ + h * BLK, BLK)], bank[:, 2 + h, :], ACT.Silu,
                                       bias=vecs[:, V_UPR:V_UPR + 1]).then_inc(s_gate, 1)
                    act.wait_ge(s_conv, b + 1)
                    act.activation(conv_x[:, ds(b * SEQ, SEQ)], state[0], ACT.Silu,
                                   bias=vecs[:, V_CONV:V_CONV + 1]).then_inc(s_x1, 1)
                act.preload_act_table_set("natural_log_exp_and_others")
                act.activation(a_neg[:, :], a_neg[:, :], ACT.Exp).then_inc(s_aneg, 1)
                with act.Fori(0, BATCH) as b:
                    for h in range(HALVES):
                        n = b * HALVES + h
                        bias = vecs[:, V_DELTA:V_DELTA + 1]
                        at = b * SEQ + h * BLK
                        act.wait_ge(s_zd, n + 1)
                        act.wait_ge(s_dl, n + 1)
                        act.activation(decay[0][:, 0:BLK], bank[:, h, :], ACT.Abs, bias=bias).then_inc(s_abs, 1)
                        act.wait_ge(s_abs, n + 1)
                        act.activation(decay[0][:, 0:BLK], decay[0][:, 0:BLK], ACT.Exp, scale=-1.0).then_inc(s_e, 1)
                        act.wait_ge(s_e, n + 1)
                        act.activation(decay[0][:, 0:BLK], decay[0][:, 0:BLK], ACT.Ln, bias=1.0).then_inc(s_sp, 1)
                        act.activation(decay[1][:, 0:BLK], bank[:, h, :], ACT.Relu, bias=bias).then_inc(s_rel, 1)
                        act.wait_ge(s_zb, n + 1)
                        act.activation(bs[:, ds(at, BLK)], bank[:, 2 + h, :], ACT.Identity,
                                       bias=vecs[:, V_B:V_B + 1]).then_inc(s_bh, 1)
                        act.wait_ge(s_zc, n + 1)
                        act.activation(cs[:, ds(at, BLK)], bank[:, 4 + h, :], ACT.Identity,
                                       bias=vecs[:, V_C:V_C + 1]).then_inc(s_ch, 1)
                act.wait_ge(s_aneg, 2)
                act.wait_ge(s_dl, 1 + NBLK)
                with act.Fori(0, BATCH) as b:
                    with act.Fori(0, STATE // SLOTS) as q:
                        for k0 in range(0, SLOTS, 2):
                            for k in (k0, k0 + 1):
                                act.wait_ge(s_scan, b * STATE + SLOTS * q + k + 1)
                                act.activation(decay[k % 2], delta[:, ds(b * SEQ, SEQ)], ACT.Exp,
                                               scale=a_neg[:, ds(SLOTS * q + k, 1)]).then_inc(s_dec, 1)
                            for k in (k0, k0 + 1):
                                u = b * STATE + SLOTS * q + k
                                act.wait_ge(s_cps, u + 1)
                                act.wait_ge(s_yacc, u + 1)
                                act.activation(term[k].rearrange("p (h t) -> p h t", h=HALVES), bank[:, 4:6, :],
                                               ACT.Copy).then_inc(s_crow, 1)

            act.wait_ge(s_small, SMALL)
            act.wait_ge(s_const, NCONST)
            ffn(0)
            mixer()
            ffn(1)

        @block.vector
        def _(dve):
            for s in (s_vec, m_cent, m_norm, s_prod, s_hid, s_xadd, s_bl, s_dl, s_scan, s_skip, s_xmix):
                dve.sem_inc(s, CREDIT[s])

            def newton(chained, var_ps, n):
                v, a, y = var_t[:, 0:n], tmp_t[:, 0:n], rstd_t[:, 0:n]
                I32 = mybir.dt.int32
                chained(lambda: dve.tensor_scalar(v, var_ps, EPS, None, ALU.add))
                chained(lambda: dve.tensor_scalar(a.bitcast(I32), v.bitcast(I32), 1, None, ALU.logical_shift_right))
                chained(lambda: dve.tensor_scalar(y.bitcast(I32), a.bitcast(I32), -1.0, float(MAGIC), ALU.mult, ALU.add))
                for _ in range(NEWTON):
                    chained(lambda: dve.tensor_tensor(a, y, y, ALU.mult))
                    chained(lambda: dve.scalar_tensor_tensor(a, a, -0.5, v, ALU.mult, ALU.mult))
                    chained(lambda: dve.scalar_tensor_tensor(y, a, 1.5, y, ALU.add, ALU.mult))

            NEWTON_STEPS = 3 + 3 * NEWTON
            ROUTE_STEPS = 27
            CHAIN = NEWTON_STEPS + ROUTE_STEPS

            def prepare(place, blk, r):
                if place == AT_CENT:
                    dve.wait_ge(s_mean, r + 1)
                    dve.tensor_tensor(cent, x[:, ds(blk * BLK, BLK)], bank[:, 7, :], ALU.subtract).then_inc(s_cent, 1)
                if place == AT_NORM:
                    dve.wait_ge(s_rstd_ps, r + 1)
                    dve.wait_ge(s_xlo, r + 1)
                    dve.tensor_tensor(xn, cent, bank[:, 7, :], ALU.mult).then_inc(s_xn, 1)

                for first, count, at, places in ((0, NEWTON_STEPS, AT_NEWTON, AT_SPREAD - AT_NEWTON),
                                                 (NEWTON_STEPS, ROUTE_STEPS, AT_ROUTE, PREP - AT_ROUTE)):
                    if at <= place < at + places:
                        lo = first + count * (place - at) // places
                        hi = first + count * (place - at + 1) // places
                        chain(r, lo, hi)

            def chain(r, lo, hi):
                n = [0]

                def chained(make, bare=False):
                    if lo <= n[0] < hi:
                        dve.wait_ge(s_vec, r * CHAIN + n[0] + 1)
                        if n[0] == 0:
                            dve.wait_ge(s_var, r + 1)
                        if n[0] == NEWTON_STEPS:
                            dve.wait_ge(s_expo, r + 1)
                        if bare:
                            dve.sem_inc(s_pass, 1)
                        make().then_inc(s_vec, 1)
                    n[0] += 1

                def tt(o, a, b, op):
                    chained(lambda: dve.tensor_tensor(o, a, b, op))

                def each(make):
                    def all_tiles():
                        for t in range(SUB):
                            i = make(t)
                        return i
                    chained(all_tiles, bare=True)

                newton(chained, bank[:, 7, 0:SUB], SUB)
                chained(lambda: dve.tensor_scalar(score, expo, 0.5, 0.5, ALU.mult, ALU.add))
                s3 = score.rearrange("p (t e) -> p t e", t=SUB)
                c3 = choice.rearrange("p (t e) -> p t e", t=SUB)
                tt(c3, s3, gate_b_sb[:, :].unsqueeze(1).broadcast_to([P, SUB, EXPERTS]), ALU.add)
                cg = choice.rearrange("p (g e) -> p g e", g=NG)
                h4 = hi4.rearrange("p (g e) -> p g e", g=NG)
                l4 = lo4.rearrange("p (g e) -> p g e", g=NG)
                n2 = mn.rearrange("p (g e) -> p g e", g=NG)
                m2 = ml.rearrange("p (g e) -> p g e", g=NG)
                tt(h4, cg[:, :, 0:4], cg[:, :, 4:8], ALU.max)
                tt(l4, cg[:, :, 0:4], cg[:, :, 4:8], ALU.min)
                for w in (2, 1):
                    tt(n2[:, :, 0:w], h4[:, :, 0:w], h4[:, :, w:2 * w], ALU.min)
                    tt(m2[:, :, 0:w], l4[:, :, 0:w], l4[:, :, w:2 * w], ALU.max)
                    tt(h4[:, :, 0:w], h4[:, :, 0:w], h4[:, :, w:2 * w], ALU.max)
                    tt(l4[:, :, 0:w], n2[:, :, 0:w], m2[:, :, 0:w], ALU.max)
                tt(gscore[:, :, 0:GROUPS], h4[:, :, 0].rearrange("p (t g) -> p t g", t=SUB),
                   l4[:, :, 0].rearrange("p (t g) -> p t g", t=SUB), ALU.add)
                each(lambda t: dve.max(top8[:, 0, t, :], gscore[:, t, :]))
                each(lambda t: dve.match_replace(gleft[:, t, :], top8[:, 0, t, :], gscore[:, t, :], GONE))
                tt(gmask[:, :].rearrange("p (t g) -> p t g", t=SUB), gscore[:, :, 0:GROUPS],
                   gleft[:, :, 0:GROUPS], ALU.not_equal)
                tt(cg, cg, gmask[:, :].unsqueeze(2).broadcast_to([P, NG, PER_GROUP]), ALU.mult)
                at = [slice(t * EXPERTS, (t + 1) * EXPERTS) for t in range(SUB)]
                each(lambda t: dve.max(top8[:, 1, t, :], choice[:, at[t]]))
                each(lambda t: dve.match_replace(rest[:, at[t]], top8[:, 1, t, :], choice[:, at[t]], GONE))
                tt(rest, rest, choice, ALU.not_equal)
                tt(score, score, rest, ALU.mult)
                chained(lambda: dve.tensor_reduce(denom[:, :], s3, AX_X, ALU.add))
                chained(lambda: dve.tensor_scalar(denom[:, :], denom[:, :], 1e-20, 1.0 / (ROUTED_SCALE * WS),
                                                  ALU.add, ALU.mult))
                chained(lambda: dve.reciprocal(denom[:, :], denom[:, :]))
                tt(s3, s3, denom[:, :].unsqueeze(2).broadcast_to([P, SUB, EXPERTS]), ALU.mult)
                chained(lambda: dve.tensor_copy(rwp[:, :, 0:EXPERTS], s3))
                tt(rwp[:, :, EXPERTS:], s3, rwp[:, :, 0:EXPERTS], ALU.subtract)
                assert n[0] == CHAIN, n[0]
                for last, ready in ((NEWTON_STEPS, s_rstd), (CHAIN, s_rwp)):
                    if lo < last <= hi:
                        dve.wait_ge(s_vec, r * CHAIN + last + 1)
                        dve.sem_inc(ready, 1)

            def hidden(u, k, block=None, routed=True):
                dve.wait_ge(s_silu, done(s_silu, u))
                dve.wait_ge(s_u, u + 1)
                dve.scalar_tensor_tensor(prod[k], bank[:, 2 + k, :], 1.0 / WS, silu_g[k], ALU.mult, ALU.mult)\
                    .then_inc(s_prod, 1)
                dve.wait_ge(s_prod, done(s_prod, u))
                dve.wait_ge(s_hlo, u + 1)
                if block is not None:
                    dve.wait_ge(s_rw, block + 1)
                if routed:
                    dve.tensor_tensor(hid[k], prod[k], bank[:, 4, :], ALU.mult).then_inc(s_hid, 1)
                else:
                    dve.tensor_scalar(hid[k], prod[k], WS, None, ALU.mult).then_inc(s_hid, 1)

            def ffn(layer):
                for place in range(PREP + 1):
                    prepare(place, 0, layer * NBLK)
                if layer == 0:
                    for c, (w, at, n, src, rows) in enumerate(chunks):
                        dve.wait_ge(s_whi, c + 1)
                        dve.scalar_tensor_tensor(w[1][0:rows, at:at + n], stage(c), WS, w[0][0:rows, at:at + n],
                                                 ALU.mult, ALU.subtract).then_inc(s_split, 1)
                base = layer * NBLK * TILES

                def tiles(blk, last=False):
                    u = base + blk * TILES
                    for j in range(HLAG, HSLOTS + PREP):
                        hidden(u + j, j % 2)
                        if not last and j >= HSLOTS:
                            prepare(j - HSLOTS, blk + 1, layer * NBLK + blk + 1)
                    with dve.Fori((HSLOTS + PREP) // 2, ROUTED_TILES // 2) as q:
                        for k in range(2):
                            hidden(u + 2 * q + k, k)
                    for j in range(ROUTED_TILES, TILES):
                        hidden(u + j, j % 2, routed=False)
                    if not last:
                        for k in range(HLAG):
                            hidden(u + TILES + k, k % 2, layer * NBLK + blk + 1 if k == 0 else None)
                    dve.wait_ge(s_dn, done(s_dn, u + TILES - 1))
                    xb = x[:, ds(blk * BLK, BLK)]
                    dve.scalar_tensor_tensor(xb, bank[:, 6, :], 0.5 / (WS * WS), xb, ALU.mult, ALU.add)\
                        .then_inc(s_xadd, 1)
                for k in range(HLAG):
                    hidden(base + k, k % 2, layer * NBLK if k == 0 else None)
                with dve.Fori(0, NBLK - 1) as blk:
                    tiles(blk)
                tiles(NBLK - 1, last=True)

            def mixer():
                lp = left[:, :].rearrange("p (b t) -> p b t", b=BATCH)
                dve.memset(lp[:, :, 0:TAPS - 1], 0.0).then_inc(s_pad, 1)
                with dve.Fori(0, NBLK // 2) as n:
                    for k in range(2):
                        at = ds((2 * n + k) * BLK, BLK)
                        dve.wait_ge(m_mean, 2 * n + k + 1)
                        dve.tensor_tensor(normed[:, at], x[:, at], bank[:, k, :], ALU.subtract).then_inc(m_cent, 1)
                count = [0]

                def chained(make):
                    make().then_inc(m_newton, 1)
                    count[0] += 1
                    dve.wait_ge(m_newton, count[0])
                dve.wait_ge(m_var, done(m_var, NBLK - 1))
                newton(chained, bank[:, 2, 0:NBLK * SUB], NBLK * SUB)
                dve.sem_inc(m_rstd, 1)
                for n in range(NBLK):
                    at = slice(n * BLK, (n + 1) * BLK)
                    dve.wait_ge(m_rstd_ps, n + 1)
                    dve.tensor_tensor(normed[:, at], normed[:, at], bank[:, 4 + n % 2, :], ALU.mult).then_inc(m_norm, 1)
                dve.wait_ge(s_pad, 1)
                with dve.Fori(0, BATCH) as b:
                    tap = [left[:, ds(b * (SEQ + TAPS - 1) + k, SEQ)] for k in range(TAPS)]
                    w = [vecs[:, V_TAP + k:V_TAP + k + 1] for k in range(TAPS)]
                    dve.wait_ge(s_lsb, done(s_lsb, b * HALVES + HALVES - 1))
                    dve.tensor_scalar(term[0], tap[0], w[0], None, ALU.mult).then_inc(s_taps, 1)
                    dve.wait_ge(s_taps, 2 * b + 1)
                    dve.scalar_tensor_tensor(term[1], tap[1], w[1], term[0], ALU.mult, ALU.add).then_inc(s_taps, 1)
                    dve.wait_ge(s_taps, 2 * b + 2)
                    dve.wait_ge(s_x1, b + 1)
                    dve.scalar_tensor_tensor(state[0], tap[2], w[2], term[1], ALU.mult, ALU.add).then_inc(s_conv, 1)
                dve.wait_ge(s_aneg, 1)
                dve.tensor_scalar(a_neg[:, :], a_neg[:, :], -1.0, None, ALU.mult).then_inc(s_aneg, 1)
                with dve.Fori(0, BATCH) as b:
                    for h in range(HALVES):
                        n = b * HALVES + h
                        at = b * SEQ + h * BLK
                        dve.wait_ge(s_rel, done(s_rel, n))
                        dve.tensor_tensor(delta[:, ds(at, BLK)], decay[0][:, 0:BLK], decay[1][:, 0:BLK], ALU.add)\
                            .then_inc(s_dl, 1)
                        dve.wait_ge(s_dl, done(s_dl, n))
                        dve.tensor_tensor(dx[:, ds(at, BLK)], delta[:, ds(at, BLK)], conv_x[:, ds(at, BLK)], ALU.mult)\
                            .then_inc(s_dxs, 1)
                        low = slice(STATE, P)
                        for dst, hi_done, bk, v in ((bs, s_bh, 2, V_B), (cs, s_ch, 4, V_C)):
                            part = dst[low, ds(at, BLK)]
                            dve.wait_ge(hi_done, n + 1)
                            dve.scalar_tensor_tensor(part, bank[low, bk + h, :], vecs[low, v:v + 1], part,
                                                     ALU.add, ALU.subtract).then_inc(s_bl, 1)
                dve.wait_ge(s_dxs, NBLK)

                def split(ap):
                    return ap.rearrange("p (h t) -> p h t", h=HALVES)

                def pair(b, n):
                    for k in range(2):
                        dbx = bank[:, 2 * k:2 * k + 2, :]
                        dve.wait_ge(s_bps, b * STATE + n + k + 1)
                        dve.tensor_tensor(dbx, dbx, split(dx[:, ds(b * SEQ, SEQ)]), ALU.mult).then_inc(s_dbx, 1)
                    for k in range(2):
                        u = b * STATE + n + k
                        dve.wait_ge(s_dbx, u + 1)
                        dve.wait_ge(s_dec, u + 1)
                        dve.wait_ge(s_term, u + 1)
                        dve.tensor_tensor_scan(state[k], decay[k],
                                               bank[:, 2 * k:2 * k + 2, :].rearrange("p h t -> p (h t)"),
                                               0.0, ALU.mult, ALU.add).then_inc(s_scan, 1)

                def finish(b):
                    at = b * SEQ
                    dve.wait_ge(s_yacc, done(s_yacc, b * STATE + STATE - 1))
                    dve.scalar_tensor_tensor(split(delta[:, ds(at, SEQ)]), split(conv_x[:, ds(at, SEQ)]),
                                             vecs[:, V_SKIP:V_SKIP + 1], bank[:, 6:8, :], ALU.mult, ALU.add)\
                        .then_inc(s_skip, 1)
                    dve.wait_ge(s_skip, done(s_skip, b))
                    dve.tensor_tensor(gate[:, ds(at, SEQ)], gate[:, ds(at, SEQ)], delta[:, ds(at, SEQ)], ALU.mult)\
                        .then_inc(s_gated, 1)

                def states(b, first=False):
                    pair(b, 0)
                    if not first:
                        finish(b - 1)
                    with dve.Fori(1, STATE // 2) as p:
                        pair(b, 2 * p)
                states(0, first=True)
                with dve.Fori(1, BATCH) as b:
                    states(b)
                finish(BATCH - 1)
                with dve.Fori(0, BATCH) as b:
                    for h in range(HALVES):
                        n = b * HALVES + h
                        xb = x[:, ds(b * SEQ + h * BLK, BLK)]
                        dve.wait_ge(s_mix, n + 1)
                        dve.scalar_tensor_tensor(xb, bank[:, h, :], vecs[:, V_DOWN:V_DOWN + 1], xb, ALU.add, ALU.add)\
                            .then_inc(s_xmix, 1)

            dve.wait_ge(s_x, 64)
            dve.wait_ge(s_small, SMALL)
            dve.wait_ge(s_const, NCONST)
            ffn(0)
            mixer()
            ffn(1)

        @block.gpsimd
        def _(pool):
            pool.sem_inc(s_xlo, CREDIT[s_xlo])
            pool.sem_inc(s_hlo, CREDIT[s_hlo])
            pool.sem_inc(s_term, CREDIT[s_term])
            pool.memset(mean_w[:, :], 1.0 / P).then_inc(s_const, 1)
            pool.memset(gscore[:, :, GROUPS:], PAD).then_inc(s_const, 1)
            for w in wg + wu:
                pool.memset(w[:, ROWS:], 0.0).then_inc(s_const, 1)
            for w in wd:
                pool.memset(w[:, (TILES - 1) * P:], 0.0).then_inc(s_const, 1)

            def ffn(layer):
                def prepare(blk, r):
                    pool.wait_ge(s_xhi, r + 1)
                    pool.tensor_tensor(xh[:, ds(blk * BLK + TOKENS, BLK)], xn, xh[:, ds(blk * BLK, BLK)],
                                       ALU.subtract).then_inc(s_xlo, 1)
                base = layer * NBLK * TILES

                def low(u, k, slot):
                    pool.wait_ge(s_hhi, u + 1)
                    pool.tensor_tensor(hid_lo[slot], hid[k], hid_hi[slot], ALU.subtract).then_inc(s_hlo, 1)

                def tiles(blk, last=False):
                    u = base + blk * TILES
                    before = 1 + (AT_TANH + 2) // HSLOTS
                    with pool.Fori(0, before) as q:
                        for k in range(HSLOTS):
                            low(u + HSLOTS * q + k, k % 2, k)
                    if not last:
                        prepare(blk + 1, layer * NBLK + blk + 1)
                    with pool.Fori(before, ROUTED_TILES // HSLOTS) as q:
                        for k in range(HSLOTS):
                            low(u + HSLOTS * q + k, k % 2, k)
                    for j in range(ROUTED_TILES, TILES):
                        low(u + j, j % 2, HSLOTS + j - ROUTED_TILES)
                prepare(0, layer * NBLK)
                with pool.Fori(0, NBLK - 1) as blk:
                    tiles(blk)
                tiles(NBLK - 1, last=True)

            ffn(0)
            with pool.Fori(0, BATCH * STATE // SLOTS) as q:
                for k in range(SLOTS):
                    u = SLOTS * q + k
                    pool.wait_ge(s_scan, done(s_scan, u))
                    pool.wait_ge(s_crow, done(s_crow, u))
                    pool.tensor_tensor(term[k], state[k % 2], term[k], ALU.mult).then_inc(s_term, 1)
            ffn(1)


_OUT = (P, TOKENS)


def kernel(**inputs):
    import numpy as np
    import concourse.bacc as bacc
    from concourse.bass_utils import run_bass_kernel_spmd as run

    a = {k.split("_", 2)[2]: np.asarray(v) for k, v in inputs.items()}
    pairs = INNER // 2
    rows = lambda w: w.reshape(EXPERTS, pairs, 2, P).transpose(1, 0, 2, 3).reshape(-1, P)
    h = P
    col = lambda v: v.reshape(P, 1)
    twice = lambda v: np.concatenate([v, v], axis=-1)
    wd_rows = np.concatenate([rows(a["Wd"].transpose(0, 2, 1)), a["Sd"].T], axis=0)
    full = (TILES - 1) * P
    row_of_expert = np.repeat(np.eye(EXPERTS, dtype=np.float16), 2, axis=1)
    one_hot = np.eye(STATE, dtype=np.float16)
    arrays = {
        "x_in": a["up_x"].reshape(TOKENS, P).T,
        "w_up": a["W_up"],
        "w_delta": a["W_delta"],
        "w_b2": twice(a["W_B"]),
        "w_c2": twice(a["W_C"]),
        "w_down": a["W_down"],
        "vecs_in": np.concatenate([col(a["b_up"][:P]), col(a["b_up"][P:]), a["conv_w"], col(a["conv_b"]),
                                   col(a["b_delta"]), col(twice(a["b_B"])), col(twice(a["b_C"])),
                                   col(a["D_skip"]), col(a["b_down"])], axis=1),
        "a_log": a["A_log"],
        "gate_wt": a["gate_w"].T,
        "gate_bias": np.broadcast_to(a["gate_bias"], (P, EXPERTS)),
        "wg_in": np.concatenate([rows(a["Wg"]), a["Sg"]], axis=0).T,
        "wu_in": np.concatenate([rows(a["Wu"]), a["Su"]], axis=0).T,
        "wd_in": wd_rows[:full].reshape(TILES - 1, P, h).transpose(1, 0, 2).reshape(P, full),
        "wd_last": wd_rows[full:],
        "row_of_expert_in": np.concatenate([row_of_expert, row_of_expert], axis=0),
        "one_hot_in": np.concatenate([one_hot, one_hot], axis=0),
        "eye_in": np.eye(P, dtype=np.float32),
        "eye16_in": np.eye(P, dtype=np.float16),
    }
    arrays = {k: np.ascontiguousarray(v) for k, v in arrays.items()}
    nc = bacc.Bacc("TRN2", target_bir_lowering=False, num_devices=1)
    args = [nc.dram_tensor(k, v.shape, mybir.dt.from_np(v.dtype), kind="ExternalInput").ap()
            for k, v in arrays.items()]
    args.append(nc.dram_tensor("out", _OUT, F32, kind="ExternalOutput").ap())
    macaron(nc, *args)
    got = run(nc, [arrays], core_ids=[0]).results[0]["out"]
    return np.ascontiguousarray(got.T).reshape(BATCH, SEQ, P)
```
